# Optimizing a Trainium2 kernel written in Bass

```python
import numpy as np
import jax
import jax.numpy as jnp

def _softmax(x, axis=-1):
    return jax.nn.softmax(x, axis=axis)

def _gelu(x):
    return jax.nn.gelu(x, approximate=True)

def _silu(x):
    return jax.nn.silu(x)

def _sigmoid(x):
    return jax.nn.sigmoid(x)

def _layernorm(x, axis=-1, eps=1e-05):
    m = jnp.mean(x, axis=axis, keepdims=True)
    v = jnp.var(x, axis=axis, keepdims=True)
    return (x - m) / jnp.sqrt(v + eps)

def _scatter_add(tgt, idx, src, axis=0):
    return tgt.at[idx].add(src)

def _segment_sum(src, seg, n):
    return jax.ops.segment_sum(src, seg, n)
kernel_name = 'mk_adaln_ffn_d1_seqx_r2_7ba202'

def setup_inputs(seed: int=0):
    np.random.seed(seed)
    _w = jnp.asarray

    def _rec_inputs():
        import jax
        import jax.numpy as jnp
        _rk = jax.random.key(seed)
        x = -0.0002071 + 1 * jax.random.normal(jax.random.fold_in(_rk, 1), (8, 512, 512), jnp.float32)
        _lenS = 512 - jax.random.randint(jax.random.fold_in(_rk, 7), (8,), 0, max(1, 512 // 4) + 1, jnp.int32)
        _lenS2 = 512 - jax.random.randint(jax.random.fold_in(_rk, 8), (8,), 0, max(1, 512 // 4) + 1, jnp.int32)
        cond_8 = jax.random.uniform(jax.random.fold_in(_rk, 11), (8, 8), jnp.float32, 0.0, 0.983423)
        return (x, cond_8)
    x, cond_8 = _rec_inputs()

    def _L0_cond_setup():
        import jax, jax.numpy as jnp
        import numpy as np
        R = 16
        ALPHA = 32.0
        SCALING = ALPHA / R
        key = jax.random.key(seed)
        ks = jax.random.split(key, 6)
        B, T, C, O, E = (16, 750, 512, 512, 8)
        x = jax.random.normal(ks[0], (B, T, C), dtype=jnp.float32)
        w = jax.random.uniform(ks[1], (B, E), dtype=jnp.float32)
        W_base = jax.random.normal(ks[2], (O, C), dtype=jnp.float32) * 0.02
        b_base = jax.random.normal(ks[3], (O,), dtype=jnp.float32) * 0.02
        As = jax.random.normal(ks[4], (E, R, C), dtype=jnp.float32) * 0.02
        Bs = jax.random.normal(ks[5], (E, O, R), dtype=jnp.float32) * 0.02
        return {'x': x, 'w': w, 'W_base': W_base, 'b_base': b_base, 'As': As, 'Bs': Bs}
    _L0_cond_all = _L0_cond_setup()
    _L0_cond_in = {k: v for k, v in _L0_cond_all.items() if k in ('W_base', 'b_base', 'As', 'Bs')}
    del _L0_cond_all

    def _L0_ffn_setup():
        import jax, jax.numpy as jnp
        import numpy as np
        D_MODEL = 512
        D_FF = 2048
        N_EXPERTS = 8
        D_EXPERT = D_FF // N_EXPERTS
        TOP_K = 2
        LB_WEIGHT = 0.01
        B, S = (4, 1024)

        def _top_k_softmax(logits, k):
            vals, _ = jax.lax.top_k(logits, k)
            thresh = vals[..., -1:]
            masked = jnp.where(logits >= thresh, logits, -jnp.inf)
            return jax.nn.softmax(masked, axis=-1)
        key = jax.random.key(seed)
        ks = jax.random.split(key, 8)
        x = jax.random.normal(ks[0], (B, S, D_MODEL), dtype=jnp.float32)
        w1 = jax.random.normal(ks[1], (N_EXPERTS, D_MODEL, D_EXPERT), dtype=jnp.float32) * (1.0 / np.sqrt(D_MODEL))
        b1 = jnp.zeros((N_EXPERTS, D_EXPERT), dtype=jnp.float32)
        w2 = jax.random.normal(ks[2], (N_EXPERTS, D_EXPERT, D_MODEL), dtype=jnp.float32) * (1.0 / np.sqrt(D_EXPERT))
        b2 = jnp.zeros((N_EXPERTS, D_MODEL), dtype=jnp.float32)
        centroids = jax.random.normal(ks[3], (N_EXPERTS, D_MODEL), dtype=jnp.float32) * 0.02
        w_route = jax.random.normal(ks[4], (N_EXPERTS, D_MODEL), dtype=jnp.float32) * (1.0 / np.sqrt(D_MODEL))
        return {'x': x, 'w1': w1, 'b1': b1, 'w2': w2, 'b2': b2, 'centroids': centroids, 'w_route': w_route}
    _L0_ffn_all = _L0_ffn_setup()
    _L0_ffn_in = {k: v for k, v in _L0_ffn_all.items() if k in ('w1', 'b1', 'w2', 'b2', 'centroids', 'w_route')}
    del _L0_ffn_all
    return {'x': x, 'cond_8': cond_8, 'L0_cond_W_base': _L0_cond_in['W_base'], 'L0_cond_b_base': _L0_cond_in['b_base'], 'L0_cond_As': _L0_cond_in['As'], 'L0_cond_Bs': _L0_cond_in['Bs'], 'L0_ffn_w1': _L0_ffn_in['w1'], 'L0_ffn_b1': _L0_ffn_in['b1'], 'L0_ffn_w2': _L0_ffn_in['w2'], 'L0_ffn_b2': _L0_ffn_in['b2'], 'L0_ffn_centroids': _L0_ffn_in['centroids'], 'L0_ffn_w_route': _L0_ffn_in['w_route']}

def reference(x, cond_8, L0_cond_W_base, L0_cond_b_base, L0_cond_As, L0_cond_Bs, L0_ffn_w1, L0_ffn_b1, L0_ffn_w2, L0_ffn_b2, L0_ffn_centroids, L0_ffn_w_route):
    import jax
    import jax.numpy as jnp

    def _L0_cond_ref(x, w, W_base, b_base, As, Bs):
        import jax, jax.numpy as jnp
        import numpy as np
        R = 16
        ALPHA = 32.0
        SCALING = ALPHA / R
        out = jnp.einsum('btc,oc->bto', x, W_base) + b_base
        h = jnp.einsum('btc,erc->bter', x, As)
        lora = jnp.einsum('bter,eor,be->bto', h, Bs, w)
        return out + lora * SCALING

    def _L0_ffn_ref(x, w1, b1, w2, b2, centroids, w_route):
        import jax, jax.numpy as jnp
        import numpy as np
        D_MODEL = 512
        D_FF = 2048
        N_EXPERTS = 8
        D_EXPERT = D_FF // N_EXPERTS
        TOP_K = 2
        LB_WEIGHT = 0.01
        B, S = (4, 1024)

        def _top_k_softmax(logits, k):
            vals, _ = jax.lax.top_k(logits, k)
            thresh = vals[..., -1:]
            masked = jnp.where(logits >= thresh, logits, -jnp.inf)
            return jax.nn.softmax(masked, axis=-1)
        eps = 1e-12
        x_norm = x / jnp.maximum(jnp.linalg.norm(x, axis=-1, keepdims=True), eps)
        c_norm = centroids / jnp.maximum(jnp.linalg.norm(centroids, axis=-1, keepdims=True), eps)
        cos_scores = jnp.einsum('bsd,ed->bse', x_norm, c_norm)
        route_scores = jnp.einsum('bsd,ed->bse', x, w_route)
        logits = cos_scores + route_scores
        gates = _top_k_softmax(logits, TOP_K)
        h = jax.nn.gelu(jnp.einsum('bsd,edh->bseh', x, w1) + b1, approximate=False)
        expert_out = jnp.einsum('bseh,ehd->bsed', h, w2) + b2
        out = jnp.einsum('bse,bsed->bsd', gates, expert_out)
        return out
    x = x + _L0_ffn_ref(_L0_cond_ref(x, cond_8, L0_cond_W_base, L0_cond_b_base, L0_cond_As, L0_cond_Bs), L0_ffn_w1, L0_ffn_b1, L0_ffn_w2, L0_ffn_b2, L0_ffn_centroids, L0_ffn_w_route)
    return x

_drawn_inputs = setup_inputs


def setup_inputs(seed=0):
    import zlib

    import numpy as np

    out = dict(_drawn_inputs(seed))
    spreads = {'L0_ffn_b1': (0.0, 0.1), 'L0_ffn_b2': (0.0, 0.1)}
    factors = {}
    for name, (base, spread) in spreads.items():
        noise = np.random.default_rng([zlib.crc32(name.encode()), seed]).standard_normal(out[name].shape)
        drawn = base * np.exp(spread * noise) if base else spread * noise
        out[name] = jnp.asarray(drawn.astype(out[name].dtype))
    for name, factor in factors.items():
        out[name] = (out[name] * factor).astype(out[name].dtype)
    return out
```

```python
from contextlib import ExitStack

import concourse.bass as bass
from concourse import mybir

P = 128
F32 = mybir.dt.float32
F32R = mybir.dt.float32r
BF16 = mybir.dt.bfloat16
FP16 = mybir.dt.float16
I32 = mybir.dt.int32
ALU = mybir.AluOpType
ACT = mybir.ActivationFunctionType
AX_X = mybir.AxisListType.X

IDENT, TRI, IOTA, TOKEN = 0, P, 2 * P, 3 * P
SCALING = 2.0
NORM_EPS = 1e-12


def wait(eng, sem, value):
    if isinstance(value, int) and value <= 0:
        return
    eng.wait_ge(sem, value)


def wait_before(eng, met, sem, value):
    if not isinstance(value, int):
        value = eng.to_reg(value)
    eng.wait_ge(*met)
    eng.wait_ge(sem, value)


def adaln_moe(nc, xT, x, consts, cond, base_wT, base_w, base_b, base_bT, lora_a, lora_b, lora_bT, weights, b1, b2, centroids, w_route, out):
    T, D = x.shape
    B = cond.shape[1]
    E = w_route.shape[0]
    F = b1.shape[1] // E * P
    KC, FC = D // P, F // P
    NT = T // P
    TB = NT // B
    SLOTS = 2 * P
    ROW = D + E
    WCOLS = weights.shape[1]
    W2_AT = WCOLS // 2
    WCH = WCOLS // NT
    LIST = NT
    E2 = 2 * E
    WIDE = D + E2
    HALF = WIDE // 2
    assert TB == 4 and KC == 4 and FC == 2 and WCH == D

    xc_rows = nc.dram_tensor("xc_rows", (T, ROW), F32, kind="Internal").ap()
    xc_tiles = xc_rows.rearrange("(n p) d -> p n d", p=P)

    with ExitStack() as ctx:
        def sb(stack, name, shape, dt):
            return stack.enter_context(nc.sbuf_tensor(name, shape, dt))

        def ps(stack, name, shape, dt=F32):
            return stack.enter_context(nc.psum_tensor(name, shape, dt))

        def sem(name):
            return ctx.enter_context(nc.semaphore(name))

        setup = ExitStack()
        sb(setup, "setup_at", [P, WCOLS - 4352], F32)
        base_nat = sb(setup, "base_nat", [P, KC, D], F32)
        b_nat = sb(setup, "b_nat", [P, KC, P], F32)
        bias_nat = sb(setup, "bias_nat", [P, KC, P], F32)
        router = sb(setup, "router", [E2, D], F32)
        iota_f = sb(setup, "iota_f", [P, P], F32)
        tri_f = sb(setup, "tri_f", [P, P], F32)
        bias_col = sb(setup, "bias_col", [P, KC], F32)
        c_norm = sb(setup, "c_norm", [E, 4], F32)
        routerT = sb(setup, "routerT", [P, KC, E2], F32)
        setup.close()
        w_hi = sb(ctx, "w_hi", [P, WCOLS], F32R)
        setup = ExitStack()
        w_raw = sb(setup, "w_raw", [P, WCOLS], F32)
        setup.close()
        w_lo = sb(ctx, "w_lo", [P, WCOLS], F32R)
        ident = sb(ctx, "ident", [P, P], F32)
        b1_sb = sb(ctx, "b1_sb", [P, E * FC], F32)
        starts = sb(ctx, "starts", [P, E + 1], I32)
        tiles_i = sb(ctx, "tiles_i", [P, E], I32)
        list_sums = sb(ctx, "list_sums", [P, E, LIST], F32)
        lists_apart = sb(ctx, "lists_apart", [P, E, LIST], I32)
        lists = sb(ctx, "lists", [P, E * LIST + LIST + 4], I32)

        gather_ix = [sb(ctx, f"gather_ix{a}", [P, 1], I32) for a in range(2)]
        gates = sb(ctx, "gates", [P, TB, E], F32)

        one = ExitStack()
        x_in = [sb(one, f"x_in{i}", [P, KC, P], F32) for i in range(2)]
        x_hi = [sb(one, f"x_hi{i}", [P, KC, P], F32R) for i in range(2)]
        x_lo = [sb(one, f"x_lo{i}", [P, KC, P], F32R) for i in range(2)]
        merged = sb(one, "merged", [P, KC, WIDE], F32)
        merged_hi = sb(one, "merged_hi", [P, KC, WIDE], F32R)
        merged_lo = sb(one, "merged_lo", [P, KC, WIDE], F32R)
        base_sb = sb(one, "base_sb", [P, KC, WIDE], F32)
        a_hi = sb(one, "a_hi", [P, D], F32R)
        setup = ExitStack()
        a_raw = sb(setup, "a_raw", [P, D], F32)
        setup.close()
        a_lo = sb(one, "a_lo", [P, D], F32R)
        b_sb = sb(one, "b_sb", [P, WIDE], F32)
        wb_hi = sb(one, "wb_hi", [P, WIDE], F32R)
        setup = ExitStack()
        wb = sb(setup, "wb", [P, WIDE], F32)
        setup.close()
        wb_lo = sb(one, "wb_lo", [P, WIDE], F32R)
        xc = [sb(one, f"xc{i}", [P, WIDE], F32) for i in range(2)]
        bias = sb(one, "bias", [P, WIDE], F32)
        squares = sb(one, "squares", [P, D], BF16)
        cond_sb = sb(one, "cond_sb", [P, B + 1], F32)
        sumsq = sb(one, "sumsq", [P, TB], F32)
        norms = sb(one, "norms", [P, TB], F32)
        inv_norm = sb(one, "inv_norm", [P, TB], F32)
        scores = sb(one, "scores", [P, TB, E2], F32)
        logits = sb(one, "logits", [P, TB, E], F32)
        mask = sb(one, "mask", [P, TB + 1, E], BF16)
        rev = sb(one, "rev", [P, NT], F32)
        rev_chosen = sb(one, "rev_chosen", [P, TB, E], F32)
        slot_base = sb(one, "slot_base", [P, TB, E], F32)
        chosen_sum = sb(one, "chosen_sum", [P, E], F32)
        slot = sb(one, "slot", [P, TB, E], I32)
        slot_row = sb(one, "slot_row", [P, TB, E], I32)
        slot_col = sb(one, "slot_col", [P, TB, E], I32)
        row_hot = sb(one, "row_hot", [P, TB, E, P], FP16)
        col_hot = sb(one, "col_hot", [P, TB, E, LIST], FP16)
        iota_h = sb(one, "iota_h", [P, P], FP16)
        token_f = sb(one, "token_f", [P, NT], F32)
        top = sb(one, "top", [P, TB, 8], F32)
        shifted = sb(one, "shifted", [P, TB, E], F32)
        powers = sb(one, "powers", [P, TB, E], F32)
        total = sb(one, "total", [P, TB], F32)
        tri = sb(one, "tri", [P, P], BF16)
        ones = sb(one, "ones", [P, P], BF16)
        ps_xc = [ps(one, f"ps_xc{i}", [P, 2, D]) for i in range(2)]
        ps_wb = ps(one, "ps_wb", [P, 2, D])
        ps_rank = ps(one, "ps_rank", [P, TB + 1, E])
        ps_list = ps(one, "ps_list", [P, E, LIST])
        one.close()

        two = ExitStack()
        rows = [sb(two, f"rows{a}", [P, ROW], F32) for a in range(2)]
        g_hi = sb(two, "g_hi", [P, KC, SLOTS], F32R)
        g_lo = sb(two, "g_lo", [P, KC, SLOTS], F32R)
        b2_sb = sb(two, "b2_sb", [P, E, D], F32)
        hid = sb(two, "hid", [P, FC, SLOTS], F32)
        h_hi = sb(two, "h_hi", [P, FC, SLOTS], F32R)
        h_lo = sb(two, "h_lo", [P, FC, SLOTS], F32R)
        y_raw = [sb(two, f"y_raw{a}", [P, D], F32) for a in range(2)]
        y_out = [sb(two, f"y_out{a}", [P, D], F32) for a in range(2)]
        gate_table = sb(two, "gate_table", [P, E * LIST + 4, E], F32)
        gate_now = sb(two, "gate_now", [P, 2], F32)
        scatter_ix = [sb(two, f"scatter_ix{a}", [P, 1], I32) for a in range(2)]
        ps_rows = ps(two, "ps_rows", [P, 2, KC, P])
        ps_hid = ps(two, "ps_hid", [P, FC, D])
        ps_y = ps(two, "ps_y", [P, 2, D])
        two.close()

        lora_in = sem("lora_in")
        small_in = sem("small_in")
        base_in = sem("base_in")
        bias_in = sem("bias_in")
        b1_in = sem("b1_in")
        router_in = sem("router_in")
        nat_in = sem("nat_in")
        base_nat_in = sem("base_nat_in")
        a_in = sem("a_in")
        x_loaded = [sem(f"x_loaded{i}") for i in range(2)]
        w_loaded = [sem(f"w_loaded{i}") for i in range(2)]
        out_init = sem("out_init")
        setup_step = sem("setup_step")
        a_split = sem("a_split")
        c_sum = sem("c_sum")
        c_root = sem("c_root")
        router_made = sem("router_made")
        router_kept = sem("router_kept")
        x_hi_done = sem("x_hi_done")
        x_lo_done = sem("x_lo_done")
        wb_done = sem("wb_done")
        wb_hi_done = sem("wb_hi_done")
        wb_lo_done = sem("wb_lo_done")
        lora_done = sem("lora_done")
        merged_done = sem("merged_done")
        merged_hi_done = sem("merged_hi_done")
        merged_lo_done = sem("merged_lo_done")
        merged_used = sem("merged_used")
        linear_done = sem("linear_done")
        xc_done = sem("xc_done")
        xc_stored = [sem(f"xc_stored{i}") for i in range(2)]
        squares_done = sem("squares_done")
        norms_done = sem("norms_done")
        scores_kept = sem("scores_kept")
        route_step = sem("route_step")
        powers_done = sem("powers_done")
        gate_step = sem("gate_step")
        gates_stored = sem("gates_stored")
        mask_done = sem("mask_done")
        ranked = sem("ranked")
        chosen_summed = sem("chosen_summed")
        slot_step = sem("slot_step")
        row_hot_done = sem("row_hot_done")
        col_hot_done = sem("col_hot_done")
        listed = sem("listed")
        list_summed = sem("list_summed")
        w_hi_done = sem("w_hi_done")
        w_lo_done = sem("w_lo_done")

        tiles_step = sem("tiles_step")
        starts_step = sem("starts_step")
        b2_in = sem("b2_in")
        first_hots = sem("first_hots")
        first_listed = sem("first_listed")
        lists_made = sem("lists_made")
        list_ready = sem("list_ready")
        ix_placed = sem("ix_placed")
        scatter_ix_done = sem("scatter_ix_done")
        gathered = [sem(f"gathered{a}") for a in range(2)]
        scattered = [sem(f"scattered{a}") for a in range(2)]
        rows_turned = sem("rows_turned")
        g_hi_done = sem("g_hi_done")
        g_lo_done = sem("g_lo_done")
        up_done = sem("up_done")
        gelu_done = sem("gelu_done")
        h_hi_done = sem("h_hi_done")
        h_lo_done = sem("h_lo_done")
        down_done = sem("down_done")
        y_biased = sem("y_biased")
        y_scaled = sem("y_scaled")

        LORA = 2 * 16
        SMALL = 3 * 16
        ROUTER = 3 * 16
        BASE_NAT = 2 * 16
        ROUTE, GATE, SLOT = 6, 4, 6

        block = ctx.enter_context(nc.Block())

        def over_batches(eng, batch):
            batch(0, 0, False)
            batch(1, 1, False)
            with eng.Fori(2, B - 1) as b:
                batch(b, 2, False)
            batch(B - 1, 2, True)

        def weigh(eng, b):
            wait(eng, lora_done, b * KC)
            wait(eng, wb_lo_done, b)
            eng.tensor_tensor(wb[:], b_sb[:], cond_sb[:, bass.ds(b, 1)].to_broadcast([P, WIDE]), ALU.mult)\
                .then_inc(wb_done, 1)

        def wb_low(eng, b):
            wait(eng, wb_hi_done, b + 1)
            eng.tensor_tensor(wb_lo[:], wb[:], wb_hi[:].bitcast(F32), ALU.subtract).then_inc(wb_lo_done, 1)

        def merged_low(eng, b, k):
            wait(eng, merged_hi_done, b * KC + k + 1)
            if 2 <= k:
                wait(eng, merged_lo_done, b * KC + k)
            eng.tensor_tensor(merged_lo[:, k, :], merged[:, k, :], merged_hi[:, k, :].bitcast(F32), ALU.subtract)\
                .then_inc(merged_lo_done, 1)

        def router_base_at(c):
            return (ps_xc[1][:, 0, 0:E2], ps_xc[1][:, 1, 0:E2], ps_list[:, 0, 0:E2],
                    ps_rank[:, 0:2, :].rearrange("p a e -> p (a e)"))[c]

        def halves(wide):
            return wide.rearrange("p (h c) -> p h c", h=2)

        def over_tiles(eng, stage, started):
            eng.wait_ge(starts_step, started)
            first = 0
            for e in range(E):
                last = eng.value_load(starts[0:1, e + 1:e + 2], min_val=0, max_val=LIST // 2 * (e + 1) - 2) + 2
                stage(first, e, e - 1)
                with eng.Fori(first + 1, last) as g:
                    stage(g, e, e)
                first = last
            return first

        @block.sync
        def _(sp):
            def load(dst, src, semaphore):
                sp.dma_start(dst, src).then_inc(semaphore, 16)

            def x_tile(n):
                return xT[bass.ds(n * P, P), :].rearrange("p (k t) -> p k t", k=KC)

            def load_weights(b, half):
                wait(sp, w_hi_done, (b - 1) * TB + 2 * half + 2)
                at = bass.ds((b * TB + 2 * half) * WCH, 2 * WCH)
                sp.dma_start(w_raw[:, at], weights[:, at]).then_inc(w_loaded[half], 16)

            chunks = "p (k o) -> p k o"
            load(router[0:E, :], centroids, router_in)
            load(router[E:E2, :], w_route, router_in)
            load(ident[:], consts[:, IDENT:IDENT + P], router_in)
            load(b_nat[:], lora_bT.rearrange(chunks, k=KC), nat_in)
            load(b_sb[:, 0:D], lora_b, lora_in)
            load(cond_sb[:, 0:B], cond, lora_in)
            load(a_raw[:], lora_a, a_in)
            load(base_nat[:], base_w.rearrange(chunks, k=KC), base_nat_in)
            load(bias_col[:], base_bT, base_nat_in)
            load(base_sb[:, :, 0:D], base_wT.rearrange(chunks, k=KC), base_in)
            load(x_in[0][:], x_tile(0), x_loaded[0])
            load(bias[:, 0:D], base_b.partition_broadcast(P), bias_in)
            load(x_in[1][:], x_tile(1), x_loaded[1])
            load_weights(0, 0)
            load(iota_f[:], consts[:, IOTA:IOTA + P], small_in)
            load(tri_f[:], consts[:, TRI:TRI + P], small_in)
            load(token_f[:], consts[:, TOKEN:TOKEN + NT], small_in)
            load(b1_sb[:], b1, b1_in)
            sp.sem_inc(gates_stored, 16)
            sp.wait_ge(x_lo_done, 1)
            load(x_in[0][:], x_tile(2), x_loaded[0])

            def batch(b, before, last):
                for t in range(TB):
                    n = b * TB + t
                    if not (last and t >= TB - 3):
                        wait(sp, x_lo_done, n + 2)
                        load(x_in[(t + 3) % 2][:], x_tile(n + 3), x_loaded[(t + 3) % 2])
                    if not (last and t >= TB - 2):
                        sp.dma_start(out[bass.ds(n * P, P), :], x[bass.ds(n * P, P), :]).then_inc(out_init, 16)
                    wait(sp, xc_done, n + 1)
                    sp.dma_start(xc_rows[bass.ds(n * P, P), 0:D], xc[t % 2][:, 0:D]).then_inc(xc_stored[t % 2], 16)
                    if t == 0:
                        load_weights(b, 1)
                    if t == 2 and not last:
                        load_weights(b + 1, 0)
                    if t == 3 and before:
                        store_gates(b - 1)

            def store_gates(b):
                wait(sp, gate_step, (b + 1) * GATE)
                sp.dma_start(xc_tiles[:, bass.ds(b * TB, TB), D:ROW], gates[:]).then_inc(gates_stored, 16)

            over_batches(sp, batch)
            sp.wait_ge(linear_done, NT)
            load(b2_sb[:], b2.rearrange("e d -> (e d)").partition_broadcast(P).rearrange("p (e d) -> p e d", e=E), b2_in)
            store_gates(B - 1)

        @block.gpsimd
        def _(pool):
            def x_low(n, t):
                wait(pool, x_hi_done, n + 1)
                pool.tensor_tensor(x_lo[t % 2][:], x_in[t % 2][:], x_hi[t % 2][:].bitcast(F32), ALU.subtract)\
                    .then_inc(x_lo_done, 1)

            x_low(0, 0)
            def weights_low(n):
                wait(pool, w_hi_done, n + 1)
                at = bass.ds(n * WCH, WCH)
                pool.tensor_tensor(w_lo[:, at], w_raw[:, at], w_hi[:, at].bitcast(F32), ALU.subtract)\
                    .then_inc(w_lo_done, 1)

            weigh(pool, 1)
            wb_low(pool, 1)

            def batch(b, before, last):
                for t in range(TB):
                    n = b * TB + t
                    if t == TB - 1 and not last:
                        weigh(pool, b + 2)
                    if not (last and t == TB - 1):
                        x_low(n + 1, t + 1)
                    if t == TB - 1 and not last:
                        merged_low(pool, b + 1, 2)
                        wb_low(pool, b + 2)
                    if before or t >= 1:
                        weights_low(n - 1)
                    if t < 2 and last:
                        at = slice((NT - 2 + t) * P, (NT - 1 + t) * P)
                        pool.dma_start(out[at, :], x[at, :]).then_inc(scattered[t], 16)

            over_batches(pool, batch)
            weights_low(NT - 1)

            pool.wait_ge(tiles_step, 3)
            pool.memset(starts[:, 0:1], -2).then_inc(starts_step, 1)
            for e in range(E):
                pool.wait_ge(starts_step, e + 1)
                pool.tensor_tensor(starts[:, e + 1:e + 2], starts[:, e:e + 1], tiles_i[:, e:e + 1], ALU.add)\
                    .then_inc(starts_step, 1)

            def gather(g, a):
                wait(pool, rows_turned, 2 * g + a - 1)
                wait_before(pool, (list_ready, 1), ix_placed, 2 * g + a + 1)
                pool.indirect_dma_start(rows[a][:], None, xc_rows,
                                        bass.IndirectOffsetOnAxis(ap=gather_ix[a][:, 0:1], axis=0))\
                    .then_inc(gathered[a], 16)

            def place_scatter_ix(g, a):
                pool.tensor_copy(scatter_ix[a][:], lists[:, bass.ds(2 * g + a, 1)]).then_inc(scatter_ix_done, 1)

            def scatter(g, a):
                pool.wait_ge(scatter_ix_done, 2 * g + 2)
                wait_before(pool, (list_ready, 1), y_scaled, 2 * g + a + 3)
                pool.indirect_dma_start(out, bass.IndirectOffsetOnAxis(ap=scatter_ix[a][:, 0:1], axis=0),
                                        y_out[a][:], None, compute_op=ALU.add).then_inc(scattered[a], 16)

            def scattered_before(g):
                for a in range(2):
                    pool.wait_ge(scattered[a], 16 * (g + 1))

            for i in range(2):
                pool.wait_ge(xc_stored[i], 16 * (NT // 2))
            pool.wait_ge(gates_stored, 16 * (B + 1))
            pool.wait_ge(out_init, 16 * (NT - 2))
            for a in range(2):
                gather(0, a)
            list_starts = [pool.value_load(starts[0:1, e:e + 1], min_val=0, max_val=LIST // 2 * e) + 2 for e in range(1, E)]
            for a in range(2):
                gather(1, a)
            pool.wait_ge(lists_made, 1)
            for e in range(1, E):
                pool.wait_ge(list_ready, e)
                pool.tensor_copy(lists[:, bass.ds(2 * list_starts[e - 1], LIST)], lists_apart[:, e, :])\
                    .then_inc(list_ready, 1)

            def stage(g, e, e_before):
                for a in range(2):
                    gather(g + 2, a)
                if not isinstance(g, int):
                    scattered_before(g - 1)
                    for a in range(2):
                        place_scatter_ix(g - 1, a)
                    for a in range(2):
                        scatter(g - 1, a)

            g = over_tiles(pool, stage, E + 1)
            scattered_before(g - 1)
            for a in range(2):
                place_scatter_ix(g - 1, a)
            for a in range(2):
                scatter(g - 1, a)
            scattered_before(g)
            for a in range(2):
                pool.wait_ge(gathered[a], 16 * (g + 2))

        @block.scalar
        def _(act):
            act.wait_ge(setup_step, 1)
            act.activation(c_norm[:, 1:2], c_norm[:, 0:1], ACT.Sqrt).then_inc(c_sum, 1)
            act.wait_ge(router_in, ROUTER)
            act.wait_ge(c_sum, 1)
            act.activation(squares[0:E, :], router[0:E, :], ACT.Square, accum_out=c_norm[:, 0:1]).then_inc(c_sum, 1)
            act.wait_ge(c_sum, 2)
            act.activation(c_norm[:, 1:2], c_norm[:, 0:1], ACT.Sqrt).then_inc(c_root, 1)
            act.wait_ge(a_in, 16)
            act.activation(a_hi[:], a_raw[:], ACT.Copy).then_inc(a_split, 1)

            def x_high(n, t):
                wait(act, x_loaded[t % 2], (n // 2 + 1) * 16 if isinstance(n, int) else (n - t) * 8 + (t // 2 + 1) * 16)
                wait(act, linear_done, n - 1)
                act.activation(x_hi[t % 2][:], x_in[t % 2][:], ACT.Copy).then_inc(x_hi_done, 1)

            def wb_high(b):
                wait(act, wb_done, b + 1)
                act.activation(wb_hi[:], wb[:], ACT.Copy).then_inc(wb_hi_done, 1)

            def merged_high(b, k):
                wait(act, merged_done, b * KC + k + 1)
                if k < KC - 1:
                    wait(act, merged_used, (b - 1) * (KC - 1) + k + 1)
                else:
                    wait(act, linear_done, b * TB)
                act.activation(merged_hi[:, k, :], merged[:, k, :], ACT.Copy).then_inc(merged_hi_done, 1)

            def weights_high(n, t, b):
                wait(act, w_loaded[t // 2], b * 16 + 16)
                at = bass.ds(n * WCH, WCH)
                act.activation(w_hi[:, at], w_raw[:, at], ACT.Copy).then_inc(w_hi_done, 1)

            def square(n, t, b):
                wait(act, xc_done, n + 1)
                wait(act, squares_done, n)
                if t == 0:
                    wait(act, norms_done, b)
                act.activation(squares[:], xc[t % 2][:, 0:D], ACT.Square, accum_out=sumsq[:, t:t + 1])\
                    .then_inc(squares_done, 1)

            def keep_scores(n, t):
                wait(act, xc_done, n + 1)
                act.activation(scores[:, t, :], xc[t % 2][:, D:WIDE], ACT.Copy).then_inc(scores_kept, 1)

            def root(b):
                wait(act, squares_done, TB * (b + 1))
                act.activation(norms[:], sumsq[:], ACT.Sqrt).then_inc(norms_done, 1)

            def power(b):
                wait(act, route_step, b * ROUTE + 6)
                act.activation(powers[:], shifted[:], ACT.Exp).then_inc(powers_done, 1)

            wb_high(0)
            x_high(0, 0)
            for k in range(KC):
                merged_high(0, k)

            wb_high(1)

            def batch(b, before, last):
                for t in range(TB):
                    n = b * TB + t
                    if not (last and t == TB - 1):
                        x_high(n + 1, t + 1)
                    if t == TB - 1 and not last:
                        for k in range(KC):
                            merged_high(b + 1, k)
                        wb_high(b + 2)
                    if before or t >= 1:
                        square(n - 1, (t - 1) % TB, b)
                    if (before or t >= 1) and t != 1:
                        keep_scores(n - 1, (t - 1) % TB)
                    if t == 0 and before:
                        root(b - 1)
                    if before or t >= 1:
                        weights_high(n - 1, (t - 1) % TB, b if t else b - 1)
                    if t == 1 and before:
                        power(b - 1)
                    if t == 1:
                        keep_scores(n - 1, 0)

            over_batches(act, batch)
            weights_high(NT - 1, TB - 1, B - 1)
            square(NT - 1, TB - 1, B - 1)
            keep_scores(NT - 1, TB - 1)
            root(B - 1)
            power(B - 1)

            def gelu(g, f, e):
                wait(act, up_done, 2 * g + f + 1)
                wait(act, h_lo_done, 2 * g)
                act.activation(hid[:, f, :], ps_hid[:, f, 0:SLOTS], ACT.Gelu, bias=b1_sb[:, e * FC + f:e * FC + f + 1])\
                    .then_inc(gelu_done, 1)

            def gathered_high(g, a):
                wait(act, rows_turned, 2 * g + a + 1)
                wait(act, up_done, 2 * g)
                act.activation(g_hi[:, :, a * P:(a + 1) * P], ps_rows[:, a, :, :], ACT.Copy).then_inc(g_hi_done, 1)

            def hidden_high(g, a):
                wait(act, gelu_done, 2 * g + 2)
                wait(act, down_done, 2 * g - 1 + a if not isinstance(g, int) else (2 * g - 1 + a if g else 0))
                act.activation(h_hi[:, :, a * P:(a + 1) * P], hid[:, :, a * P:(a + 1) * P], ACT.Copy)\
                    .then_inc(h_hi_done, 1)

            def scale(g, a):
                act.wait_ge(y_biased, 2 * g + a + 3)
                act.wait_ge(scattered[a], 16 * (g + 1))
                act.activation(y_out[a][:], y_raw[a][:], ACT.Identity, scale=gate_now[:, a:a + 1])\
                    .then_inc(y_scaled, 1)

            act.wait_ge(b1_in, 16)
            act.sem_inc(y_scaled, 2)
            for a in range(2):
                gathered_high(0, a)

            def stage(g, e, e_before):
                for f in range(FC):
                    gelu(g, f, e)
                for a in range(2):
                    gathered_high(g + 1, a)
                for a in range(2):
                    hidden_high(g, a)
                    if not isinstance(g, int):
                        scale(g - 1, a)

            g = over_tiles(act, stage, E + 1)
            for a in range(2):
                scale(g - 1, a)

        @block.vector
        def _(vec):
            def stepper(semaphore, start):
                count = [0]

                def step(instruction):
                    instruction.then_inc(semaphore, 1)
                    count[0] += 1
                    vec.wait_ge(semaphore, start + count[0])
                return step

            setup = stepper(setup_step, 0)
            step = setup
            step(vec.memset(c_norm[:], 0.0))
            step(vec.memset(cond_sb[:, B:B + 1], 0.0))
            step(vec.memset(ones[:], 1.0))
            step(vec.memset(mask[:, TB, :], 0.0))
            step(vec.memset(chosen_sum[:], 0.0))
            step(vec.memset(list_sums[:], 0.0))
            step(vec.memset(lists[:], 0))

            def merge(b, k):
                wait(vec, lora_done, b * KC + k + 1)
                wait(vec, merged_lo_done, (b - 1) * KC + k + 1)
                vec.tensor_tensor(halves(merged[:, k, :]), ps_wb[:, :, 0:HALF], halves(base_sb[:, k, :]), ALU.add)\
                    .then_inc(merged_done, 1)

            def linear_out(n, t):
                wait(vec, linear_done, n + 1)
                wait(vec, squares_done, n - 1)
                wait(vec, scores_kept, n - 1)
                wait(vec, xc_stored[t % 2], n // 2 * 16 if isinstance(n, int) else (n - t) * 8 + t // 2 * 16)
                vec.tensor_tensor(halves(xc[t % 2][:]), ps_xc[t % 2][:, :, 0:HALF], halves(bias[:]), ALU.add)\
                    .then_inc(xc_done, 1)

            def norm(b):
                step = stepper(route_step, b * ROUTE)
                wait(vec, norms_done, b + 1)
                step(vec.tensor_scalar(inv_norm[:], norms[:], NORM_EPS, None, ALU.max))
                step(vec.reciprocal(inv_norm[:], inv_norm[:]))

            def choose(b):
                step = stepper(route_step, b * ROUTE + 2)
                wait(vec, scores_kept, TB * (b + 1))
                step(vec.tensor_tensor(logits[:], scores[:, :, 0:E],
                                       inv_norm[:].unsqueeze(2).to_broadcast([P, TB, E]), ALU.mult))
                vec.tensor_tensor(logits[:], logits[:], scores[:, :, E:E2], ALU.add).then_inc(route_step, 1)
                wait_before(vec, (small_in, SMALL), route_step, b * ROUTE + 4)
                for t in range(TB):
                    last = vec.max(top[:, t, :], logits[:, t, :])
                step = stepper(route_step, b * ROUTE + 4)
                step(last)
                wait(vec, ranked, b)
                vec.tensor_tensor(mask[:, 0:TB, :], logits[:], top[:, :, 1:2].to_broadcast([P, TB, E]), ALU.is_ge)\
                    .then_inc(mask_done, 1)
                step(vec.tensor_tensor(shifted[:], logits[:], top[:, :, 0:1].to_broadcast([P, TB, E]), ALU.subtract))
                vec.wait_ge(mask_done, b + 1)

            def gate(b):
                step = stepper(gate_step, b * GATE)
                wait(vec, powers_done, b + 1)
                step(vec.tensor_tensor(powers[:], powers[:], mask[:, 0:TB, :], ALU.mult))
                step(vec.tensor_reduce(total[:], powers[:], AX_X, ALU.add))
                step(vec.reciprocal(total[:], total[:]))
                wait(vec, gates_stored, 16 * (b + 1))
                step(vec.tensor_tensor(gates[:], powers[:], total[:].unsqueeze(2).to_broadcast([P, TB, E]), ALU.mult))

            def base_slots(b):
                step = stepper(slot_step, b * SLOT)
                at = bass.ds(b * TB, TB)
                step(vec.tensor_tensor(rev_chosen[:], rev[:, at].unsqueeze(2).to_broadcast([P, TB, E]),
                                       mask[:, 0:TB, :], ALU.mult))
                step(vec.tensor_tensor(slot_base[:], rev[:, at].unsqueeze(2).to_broadcast([P, TB, E]),
                                       rev_chosen[:], ALU.subtract))
                step(vec.tensor_tensor(slot_base[:], slot_base[:],
                                       chosen_sum[:].unsqueeze(1).to_broadcast([P, TB, E]), ALU.add))

            def slots(b):
                step = stepper(slot_step, b * SLOT + 3)
                wait(vec, ranked, b + 1)
                wait(vec, row_hot_done, b * TB)
                step(vec.tensor_tensor(slot[:], ps_rank[:, 0:TB, :], slot_base[:], ALU.add))
                step(vec.tensor_scalar(slot_row[:], slot[:], P - 1, None, ALU.bitwise_and))
                step(vec.tensor_scalar(slot_col[:], slot[:], P.bit_length() - 1, None, ALU.logical_shift_right))
                vec.tensor_tensor(chosen_sum[:], chosen_sum[:], ps_rank[:, TB, :], ALU.add).then_inc(chosen_summed, 1)
                vec.wait_ge(chosen_summed, b + 1)

            def row_one_hot(b, t, experts=slice(0, E)):
                wait(vec, slot_step, b * SLOT + 6)
                shape = [P, experts.stop - experts.start, P]
                vec.tensor_tensor(row_hot[:, t, experts, :], iota_h[:].unsqueeze(1).to_broadcast(shape),
                                  slot_row[:, t, experts].unsqueeze(2).to_broadcast(shape), ALU.is_equal)\
                    .then_inc(row_hot_done, 1)

            def col_one_hot(b, experts=slice(0, E)):
                wait(vec, listed, b)
                shape = [P, TB, experts.stop - experts.start, LIST]
                vec.tensor_tensor(col_hot[:, :, experts, :], iota_h[:, 0:LIST].unsqueeze(1).unsqueeze(1).to_broadcast(shape),
                                  slot_col[:, :, experts].unsqueeze(3).to_broadcast(shape), ALU.is_equal)\
                    .then_inc(col_hot_done, 1)

            def col_times_token(b, t, experts=slice(0, E)):
                wait(vec, col_hot_done, b * (TB + 1) + 1)
                vec.tensor_scalar(col_hot[:, t, experts, :], col_hot[:, t, experts, :], token_f[:, bass.ds(b * TB + t, 1)],
                                  None, ALU.mult).then_inc(col_hot_done, 1)

            def sum_lists(b):
                wait(vec, listed, b + 1)
                wait(vec, list_summed, b + 1)
                vec.tensor_tensor(list_sums[:], list_sums[:], ps_list[:], ALU.add).then_inc(list_summed, 1)

            vec.sem_inc(list_summed, 1)
            vec.wait_ge(lora_in, LORA)
            step(vec.tensor_scalar(cond_sb[:, 0:B], cond_sb[:, 0:B], SCALING, None, ALU.mult))
            vec.wait_ge(c_root, 1)
            step(vec.tensor_scalar(c_norm[:, 2:3], c_norm[:, 1:2], NORM_EPS, None, ALU.max))
            step(vec.reciprocal(c_norm[:, 3:4], c_norm[:, 2:3]))
            step(vec.tensor_scalar(router[0:E, :], router[0:E, :], c_norm[:, 3:4], None, ALU.mult))
            vec.wait_ge(router_made, 1)
            vec.tensor_copy(routerT[:], ps_list[:, 0:2, :].rearrange("p a c -> p (a c)")
                            .rearrange("p (k e) -> p k e", k=KC)).then_inc(router_kept, 1)
            vec.wait_ge(router_made, 2)
            vec.tensor_copy(b_sb[:, D:WIDE], ps_xc[0][:, 0, 0:E2]).then_inc(router_kept, 1)
            vec.wait_ge(router_kept, 2)
            weigh(vec, 0)
            wb_low(vec, 0)
            vec.wait_ge(a_split, 1)
            step(vec.tensor_tensor(a_lo[:], a_raw[:], a_hi[:].bitcast(F32), ALU.subtract))
            vec.wait_ge(base_nat_in, BASE_NAT)
            step(vec.tensor_copy(bias_nat[:], bias_col[:].unsqueeze(2).to_broadcast([P, KC, P])))
            vec.wait_ge(base_in, 16)
            for k in range(KC):
                vec.wait_ge(router_made, 3 + k)
                vec.tensor_copy(base_sb[:, k, D:WIDE], router_base_at(k)).then_inc(router_kept, 1)
                vec.wait_ge(router_kept, 3 + k)
                merge(0, k)
                if k:
                    merged_low(vec, 0, k - 1)
            merged_low(vec, 0, KC - 1)
            vec.wait_ge(router_made, 3 + KC)
            vec.tensor_copy(bias[:, D:WIDE], ps_xc[1][:, 0, 0:E2]).then_inc(router_kept, 1)
            vec.wait_ge(router_kept, 3 + KC)
            vec.wait_ge(small_in, SMALL)
            step(vec.tensor_copy(tri[:], tri_f[:]))
            step(vec.tensor_copy(iota_h[:], iota_f[:]))
            step(vec.tensor_scalar(rev[:], token_f[:], -1.0, float(T // 2 - 1), ALU.mult, ALU.add))
            vec.wait_ge(bias_in, 16)

            def batch(b, before, last):
                if before == 2:
                    row_one_hot(b - 2, 0)
                    row_one_hot(b - 2, 1)
                linear_out(b * TB, 0)
                if not last:
                    merge(b + 1, 0)
                if before == 2:
                    row_one_hot(b - 2, 2)
                    row_one_hot(b - 2, 3)
                if before:
                    norm(b - 1)
                    choose(b - 1)
                    base_slots(b - 1)
                linear_out(b * TB + 1, 1)
                if before:
                    slots(b - 1)
                if not last:
                    merge(b + 1, 1)
                if before:
                    gate(b - 1)
                if before == 2:
                    sum_lists(b - 2)
                if not last:
                    merge(b + 1, 2)
                    linear_out(b * TB + 2, 2)
                    merge(b + 1, 3)
                if before:
                    col_one_hot(b - 1)
                if not last:
                    merged_low(vec, b + 1, 0)
                    merged_low(vec, b + 1, 1)
                    merged_low(vec, b + 1, 3)
                    linear_out(b * TB + 3, 3)
                if last:
                    row_one_hot(b - 1, 0)
                    linear_out(b * TB + 2, 2)
                    row_one_hot(b - 1, 1)
                    row_one_hot(b - 1, 2)
                    linear_out(b * TB + 3, 3)
                    row_one_hot(b - 1, 3)
                if before:
                    for i in range(TB):
                        col_times_token(b - 1, i)

            over_batches(vec, batch)
            norm(B - 1)
            choose(B - 1)
            base_slots(B - 1)
            slots(B - 1)
            sum_lists(B - 2)
            now = slice((B - 1) * TB, B * TB)
            shape = [P, TB, LIST]
            step = stepper(first_hots, 0)
            step(vec.tensor_tensor(col_hot[:, :, 0, :], iota_h[:, 0:LIST].unsqueeze(1).to_broadcast(shape),
                                   slot_col[:, :, 0].unsqueeze(2).to_broadcast(shape), ALU.is_equal))
            step(vec.tensor_tensor(col_hot[:, :, 0, :], col_hot[:, :, 0, :],
                                   token_f[:, now].unsqueeze(2).to_broadcast(shape), ALU.mult))
            shape = [P, TB, P]
            step(vec.tensor_tensor(row_hot[:, :, 0, :], iota_h[:].unsqueeze(1).to_broadcast(shape),
                                   slot_row[:, :, 0].unsqueeze(2).to_broadcast(shape), ALU.is_equal))
            gate(B - 1)
            vec.wait_ge(first_listed, 1)
            vec.tensor_tensor(list_sums[:, 0, :], list_sums[:, 0, :], ps_list[:, 0, :], ALU.add).then_inc(list_summed, 1)
            vec.wait_ge(list_summed, B + 1)
            vec.tensor_scalar(lists[:, 0:LIST], list_sums[:, 0, :], float(T // 2), None, ALU.add).then_inc(list_ready, 1)
            vec.wait_ge(list_ready, 1)
            for a in range(2):
                vec.tensor_copy(gather_ix[a][:], lists[:, a:a + 1]).then_inc(ix_placed, 1)
            step = stepper(tiles_step, 0)
            step(vec.tensor_scalar(tiles_i[:], chosen_sum[:], float(SLOTS - 1), None, ALU.add))
            step(vec.tensor_scalar(tiles_i[:], tiles_i[:], SLOTS.bit_length() - 1, None, ALU.logical_shift_right))
            step(vec.tensor_scalar(tiles_i[:], tiles_i[:], 2.0, None, ALU.max))
            others = slice(1, E)
            col_one_hot(B - 1, others)
            for t in range(TB):
                col_times_token(B - 1, t, others)
            for t in range(TB):
                row_one_hot(B - 1, t, others)
            def keep_gates(g, a):
                vec.wait_ge(gathered[a], 16 * (g + 1))
                vec.tensor_copy(gate_table[:, bass.ds(2 * g + a, 1), :], rows[a][:, D:ROW].unsqueeze(1))
                vec.tensor_copy(gather_ix[a][:], lists[:, bass.ds(2 * g + 2 + a, 1)]).then_inc(ix_placed, 1)

            def gathered_low(g, a):
                wait(vec, g_hi_done, 2 * g + a + 1)
                vec.tensor_tensor(g_lo[:, :, a * P:(a + 1) * P], ps_rows[:, a, :, :],
                                  g_hi[:, :, a * P:(a + 1) * P].bitcast(F32), ALU.subtract).then_inc(g_lo_done, 1)

            def hidden_low(g, a):
                wait(vec, h_hi_done, 2 * g + a + 1)
                half = slice(a * P, (a + 1) * P)
                vec.tensor_tensor(h_lo[:, :, half], hid[:, :, half], h_hi[:, :, half].bitcast(F32), ALU.subtract)\
                    .then_inc(h_lo_done, 1)

            def add_bias(g, a, e):
                vec.wait_ge(y_scaled, 2 * g + a + 1)
                vec.tensor_copy(gate_now[:, a:a + 1], gate_table[:, bass.ds(2 * g + a, 1), e])
                vec.wait_ge(down_done, 2 * g + a + 1)
                vec.tensor_tensor(y_raw[a][:], ps_y[:, a, :], b2_sb[:, e, :], ALU.add).then_inc(y_biased, 1)

            vec.sem_inc(y_biased, 2)
            for a in range(2):
                keep_gates(0, a)
            for a in range(2):
                gathered_low(0, a)
            vec.wait_ge(listed, B)
            vec.tensor_tensor(list_sums[:, others, :], list_sums[:, others, :], ps_list[:, others, :], ALU.add)\
                .then_inc(list_summed, 1)
            vec.wait_ge(list_summed, B + 2)
            vec.tensor_scalar(lists_apart[:], list_sums[:], float(T // 2), None, ALU.add).then_inc(lists_made, 1)
            vec.wait_ge(b2_in, 16)
            vec.wait_ge(list_ready, E)

            def stage(g, e, e_before):
                for a in range(2):
                    keep_gates(g + 1, a)
                for a in range(2):
                    gathered_low(g + 1, a)
                for a in range(2):
                    if not isinstance(g, int):
                        add_bias(g - 1, a, e_before)
                    hidden_low(g, a)

            g = over_tiles(vec, stage, E + 1)
            for a in range(2):
                add_bias(g - 1, a, E - 1)

        @block.tensor
        def _(pe):
            def split_product(dst, sta, mov, start, stop):
                pe.matmul(dst, sta[0], mov[0], start=start, stop=False)
                pe.matmul(dst, sta[0], mov[1], start=False, stop=False)
                return pe.matmul(dst, sta[1], mov[0], start=False, stop=stop)

            def wide_product(dst, sta, mov, start, stop):
                for i, (s, m) in enumerate(((0, 0), (0, 1), (1, 0))):
                    for h in range(2):
                        last = pe.matmul(dst[:, h, 0:HALF], sta[s], mov[m][:, h * HALF:(h + 1) * HALF],
                                         start=start and i == 0, stop=stop and i == 2)
                return last

            def adapters(b, k):
                if k == 0:
                    wait(pe, wb_lo_done, b + 1)
                wait(pe, merged_done, b * KC + k)
                cols = slice(k * P, (k + 1) * P)
                wide_product(ps_wb, (a_hi[:, cols], a_lo[:, cols]), (wb_hi, wb_lo), True, True)\
                    .then_inc(lora_done, 1)

            def linear(n, b, t, last_batch):
                wait(pe, x_lo_done, n + 1)
                wait(pe, xc_done, n - 1)
                for k in range(KC):
                    if t == 0:
                        wait(pe, merged_lo_done, b * KC + k + 1)
                    if t == 2 and k == 2 and not last_batch:
                        adapters(b + 1, 2)
                    last = wide_product(ps_xc[t % 2], (x_hi[t % 2][:, k, :], x_lo[t % 2][:, k, :]),
                                        (merged_hi[:, k, :], merged_lo[:, k, :]), k == 0, k == KC - 1)
                    if t == TB - 1 and k < KC - 1:
                        last.then_inc(merged_used, 1)
                last.then_inc(linear_done, 1)

            def rank_tokens(b):
                wait(pe, mask_done, b + 1)
                wait(pe, chosen_summed, b)
                pe.matmul(ps_rank[:], tri[:], mask[:], start=True, stop=False)
                for i in range(1, TB + 1):
                    last = pe.matmul(ps_rank[:, i:TB + 1, :], ones[:], mask[:, 0:TB + 1 - i, :],
                                     start=False, stop=(i == TB))
                last.then_inc(ranked, 1)

            def make_lists(b, experts=range(E)):
                wait(pe, row_hot_done, (b + 1) * TB)
                wait(pe, col_hot_done, (b + 1) * (TB + 1))
                wait(pe, list_summed, b + 1)
                for e in experts:
                    for t in range(TB):
                        last = pe.matmul(ps_list[:, e, :], row_hot[:, t, e, :], col_hot[:, t, e, :],
                                         start=(t == 0), stop=(t == TB - 1))
                last.then_inc(listed, 1)

            pe.wait_ge(setup_step, 11)
            turned = ps_list[:, 0:2, :].rearrange("p a c -> p (a c)")
            for k in range(KC):
                last = pe.transpose(turned[:, k * E2:(k + 1) * E2], router[:, k * P:(k + 1) * P], ident[0:E2, 0:E2])
            last.then_inc(router_made, 1)
            pe.wait_ge(router_kept, 1)
            pe.wait_ge(nat_in, 16)
            for k in range(KC):
                last = pe.matmul(ps_xc[0][:, 0, 0:E2], b_nat[:, k, :], routerT[:, k, :], start=(k == 0), stop=(k == KC - 1))
            last.then_inc(router_made, 1)
            pe.wait_ge(base_nat_in, BASE_NAT)
            for c in range(KC):
                for k in range(KC):
                    last = pe.matmul(router_base_at(c), base_nat[:, k, c * P:(c + 1) * P], routerT[:, k, :],
                                     start=(k == 0), stop=(k == KC - 1))
                last.then_inc(router_made, 1)
                if c == 0:
                    pe.wait_ge(setup_step, 12)
                adapters(0, c)
            pe.wait_ge(setup_step, 13)
            for k in range(KC):
                last = pe.matmul(ps_xc[1][:, 0, 0:E2], bias_nat[:, k, :], routerT[:, k, :], start=(k == 0), stop=(k == KC - 1))
            last.then_inc(router_made, 1)

            def batch(b, before, last):
                for t in range(TB):
                    n = b * TB + t
                    if t == 2 and before == 2:
                        make_lists(b - 2)
                    if t == 1 and not before:
                        pe.wait_ge(router_kept, 3 + KC)
                    linear(n, b, t, last)
                    if t < 2 and not last:
                        adapters(b + 1, t)
                    if t == 2 and not last:
                        adapters(b + 1, 3)
                    if t == 1 and before:
                        rank_tokens(b - 1)

            over_batches(pe, batch)
            make_lists(B - 2)
            rank_tokens(B - 1)
            pe.wait_ge(first_hots, 3)
            pe.wait_ge(list_summed, B)
            for t in range(TB):
                last = pe.matmul(ps_list[:, 0, :], row_hot[:, t, 0, :], col_hot[:, t, 0, :], start=(t == 0), stop=(t == TB - 1))
            last.then_inc(first_listed, 1)
            pe.wait_ge(list_summed, B + 1)
            def turn_rows(g, a):
                pe.wait_ge(gathered[a], 16 * (g + 1))
                wait(pe, g_lo_done, 2 * g + a - 1)
                for k in range(KC):
                    last = pe.transpose(ps_rows[:, a, k, :], rows[a][:, k * P:(k + 1) * P], ident[:])
                last.then_inc(rows_turned, 1)

            def up(g, e):
                wait(pe, g_lo_done, 2 * g + 2)
                for f in range(FC):
                    wait(pe, gelu_done, 2 * g - 1 + f if not isinstance(g, int) or g else 0)
                    for k in range(KC):
                        at = e * KC * F + k * F + f * P
                        last = split_product(ps_hid[:, f, 0:SLOTS], (w_hi[:, at:at + P], w_lo[:, at:at + P]),
                                             (g_hi[:, k, :], g_lo[:, k, :]), k == 0, k == KC - 1)
                    last.then_inc(up_done, 1)

            def down(g, a, e):
                pe.wait_ge(h_lo_done, 2 * g + a + 1)
                pe.wait_ge(y_biased, 2 * g + a + 1)
                half = slice(a * P, (a + 1) * P)
                for f in range(FC):
                    at = W2_AT + e * FC * D + f * D
                    last = split_product(ps_y[:, a, :], (h_hi[:, f, half], h_lo[:, f, half]),
                                         (w_hi[:, at:at + D], w_lo[:, at:at + D]), f == 0, f == FC - 1)
                last.then_inc(down_done, 1)

            pe.wait_ge(xc_done, NT)
            for a in range(2):
                turn_rows(0, a)
            make_lists(B - 1, range(1, E))
            pe.wait_ge(list_summed, B + 2)

            def stage(g, e, e_before):
                up(g, e)
                for a in range(2):
                    turn_rows(g + 1, a)
                if not isinstance(g, int):
                    for a in range(2):
                        down(g - 1, a, e_before)

            g = over_tiles(pe, stage, E + 1)
            for a in range(2):
                down(g - 1, a, E - 1)


def kernel(**inputs):
    import numpy as np
    import concourse.bacc as bacc
    from concourse.bass_utils import run_bass_kernel_spmd

    x = np.asarray(inputs["x"])
    Bn, S, D = x.shape
    T = Bn * S
    w_base = np.asarray(inputs["L0_cond_W_base"])
    a_mat = np.asarray(inputs["L0_cond_As"])
    b_mat = np.asarray(inputs["L0_cond_Bs"])
    w1 = np.asarray(inputs["L0_ffn_w1"])
    w2 = np.asarray(inputs["L0_ffn_w2"])
    E, _, F = w1.shape
    rank = a_mat.shape[1]
    KC, FC, NT = D // P, F // P, T // P

    consts = np.zeros((P, 3 * P + NT), np.float32)
    consts[:, IDENT:IDENT + P] = np.eye(P)
    consts[:, TRI:TRI + P] = np.triu(np.ones((P, P)), 1)
    consts[:, IOTA:IOTA + P] = np.arange(P)
    consts[:, TOKEN:TOKEN + NT] = (np.arange(T) - T // 2).reshape(NT, P).T

    arrays = {
        "xT": x.reshape(NT, P, KC, P).transpose(0, 3, 2, 1).reshape(T, D),
        "x": x.reshape(T, D),
        "consts": consts,
        "cond": np.repeat(np.asarray(inputs["cond_8"]).T, rank, axis=0),
        "base_wT": w_base.T.reshape(KC, P, D).transpose(1, 0, 2).reshape(P, KC * D),
        "base_w": w_base.reshape(KC, P, D).transpose(1, 0, 2).reshape(P, KC * D),
        "base_b": np.asarray(inputs["L0_cond_b_base"]),
        "base_bT": np.asarray(inputs["L0_cond_b_base"]).reshape(KC, P).T,
        "lora_a": a_mat.reshape(E * rank, D),
        "lora_b": b_mat.transpose(0, 2, 1).reshape(E * rank, D),
        "lora_bT": b_mat.transpose(1, 0, 2).reshape(KC, P, E * rank).transpose(1, 0, 2).reshape(P, KC * E * rank),
        "weights": np.concatenate([
            w1.reshape(E, KC, P, F).transpose(2, 0, 1, 3).reshape(P, E * KC * F),
            w2.reshape(E, FC, P, D).transpose(2, 0, 1, 3).reshape(P, E * FC * D)], axis=1),
        "b1": np.asarray(inputs["L0_ffn_b1"]).reshape(E, FC, P).transpose(2, 0, 1).reshape(P, E * FC),
        "b2": np.asarray(inputs["L0_ffn_b2"]),
        "centroids": np.asarray(inputs["L0_ffn_centroids"]),
        "w_route": np.asarray(inputs["L0_ffn_w_route"]),
    }
    nc = bacc.Bacc("TRN2", target_bir_lowering=False, num_devices=1)
    feeds, args = {}, []
    for name, a in arrays.items():
        a = np.ascontiguousarray(a)
        feeds[f"in_{name}"] = a
        args.append(nc.dram_tensor(f"in_{name}", a.shape, mybir.dt.from_np(a.dtype), kind="ExternalInput").ap())
    out = nc.dram_tensor("out_0", (T, D), F32, kind="ExternalOutput").ap()
    adaln_moe(nc, *args, out)
    r = run_bass_kernel_spmd(nc, [feeds], core_ids=[0])
    return r.results[0]["out_0"].reshape(Bn, S, D)
```

```python
from contextlib import ExitStack

import concourse.bass as bass
from concourse import mybir

P = 128
F32 = mybir.dt.float32
F32R = mybir.dt.float32r
BF16 = mybir.dt.bfloat16
FP16 = mybir.dt.float16
I32 = mybir.dt.int32
ALU = mybir.AluOpType
ACT = mybir.ActivationFunctionType
AX_X = mybir.AxisListType.X

IDENT, TRI, IOTA, TOKEN = 0, P, 2 * P, 3 * P
SCALING = 2.0
NORM_EPS = 1e-12


def wait(eng, sem, value):
    if isinstance(value, int) and value <= 0:
        return
    eng.wait_ge(sem, value)


def wait_before(eng, met, sem, value):
    if not isinstance(value, int):
        value = eng.to_reg(value)
    eng.wait_ge(*met)
    eng.wait_ge(sem, value)


def adaln_moe(nc, xT, x, consts, cond, base_wT, base_w, base_b, base_bT, lora_a, lora_b, lora_bT, weights, b1, b2, centroids, w_route, out):
    T, D = x.shape
    B = cond.shape[1]
    E = w_route.shape[0]
    F = b1.shape[1] // E * P
    KC, FC = D // P, F // P
    NT = T // P
    TB = NT // B
    SLOTS = 2 * P
    ROW = D + E
    WCOLS = weights.shape[1]
    W2_AT = WCOLS // 2
    WCH = WCOLS // NT
    LIST = NT
    E2 = 2 * E
    WIDE = D + E2
    HALF = WIDE // 2
    assert TB == 4 and KC == 4 and FC == 2 and WCH == D

    xc_rows = nc.dram_tensor("xc_rows", (T, ROW), F32, kind="Internal").ap()
    xc_tiles = xc_rows.rearrange("(n p) d -> p n d", p=P)

    with ExitStack() as ctx:
        def sb(stack, name, shape, dt):
            return stack.enter_context(nc.sbuf_tensor(name, shape, dt))

        def ps(stack, name, shape, dt=F32):
            return stack.enter_context(nc.psum_tensor(name, shape, dt))

        def sem(name):
            return ctx.enter_context(nc.semaphore(name))

        setup = ExitStack()
        SETUP = KC * D + 2 * KC * P + D + 2 * P + KC + 4 + KC * E2 + 64
        sb(setup, "w_hi_before_setup", [P, WCOLS - SETUP], F32)
        base_nat = sb(setup, "base_nat", [P, KC, D], F32)
        b_nat = sb(setup, "b_nat", [P, KC, P], F32)
        bias_nat = sb(setup, "bias_nat", [P, KC, P], F32)
        router = sb(setup, "router", [E2, D], F32)
        iota_f = sb(setup, "iota_f", [P, P], F32)
        tri_f = sb(setup, "tri_f", [P, P], F32)
        bias_col = sb(setup, "bias_col", [P, KC], F32)
        c_norm = sb(setup, "c_norm", [E, 4], F32)
        routerT = sb(setup, "routerT", [P, KC, E2], F32)
        setup.close()
        w_hi = sb(ctx, "w_hi", [P, WCOLS], F32R)
        setup = ExitStack()
        w_raw = sb(setup, "w_raw", [P, WCOLS], F32)
        setup.close()
        w_lo = sb(ctx, "w_lo", [P, WCOLS], F32R)
        ident = sb(ctx, "ident", [P, P], F32)
        b1_sb = sb(ctx, "b1_sb", [P, E * FC], F32)
        starts = sb(ctx, "starts", [P, E + 1], I32)
        tiles_i = sb(ctx, "tiles_i", [P, E], I32)
        list_sums = sb(ctx, "list_sums", [P, E, LIST], F32)
        lists_apart = sb(ctx, "lists_apart", [P, E, LIST], I32)
        lists = sb(ctx, "lists", [P, E * LIST + LIST + 4], I32)

        gather_ix = [sb(ctx, f"gather_ix{a}", [P, 1], I32) for a in range(2)]
        gates = sb(ctx, "gates", [P, TB, E], F32)

        one = ExitStack()
        x_in = [sb(one, f"x_in{i}", [P, KC, P], F32) for i in range(2)]
        x_hi = [sb(one, f"x_hi{i}", [P, KC, P], F32R) for i in range(2)]
        x_lo = [sb(one, f"x_lo{i}", [P, KC, P], F32R) for i in range(2)]
        merged = sb(one, "merged", [P, KC, WIDE], F32)
        merged_hi = sb(one, "merged_hi", [P, KC, WIDE], F32R)
        merged_lo = sb(one, "merged_lo", [P, KC, WIDE], F32R)
        base_sb = sb(one, "base_sb", [P, KC, WIDE], F32)
        a_hi = sb(one, "a_hi", [P, D], F32R)
        setup = ExitStack()
        a_raw = sb(setup, "a_raw", [P, D], F32)
        setup.close()
        a_lo = sb(one, "a_lo", [P, D], F32R)
        b_sb = sb(one, "b_sb", [P, WIDE], F32)
        wb_hi = sb(one, "wb_hi", [P, WIDE], F32R)
        setup = ExitStack()
        wb = sb(setup, "wb", [P, WIDE], F32)
        setup.close()
        wb_lo = sb(one, "wb_lo", [P, WIDE], F32R)
        xc = [sb(one, f"xc{i}", [P, WIDE], F32) for i in range(2)]
        bias = sb(one, "bias", [P, WIDE], F32)
        squares = sb(one, "squares", [P, D], BF16)
        cond_sb = sb(one, "cond_sb", [P, B + 1], F32)
        sumsq = sb(one, "sumsq", [P, TB], F32)
        norms = sb(one, "norms", [P, TB], F32)
        half = sb(one, "half", [P, TB], F32)
        inv_norm = sb(one, "inv_norm", [P, TB], F32)
        scores = sb(one, "scores", [P, TB, E2], F32)
        logits = sb(one, "logits", [P, TB, E], F32)
        mask = sb(one, "mask", [P, TB + 1, E], BF16)
        rev = sb(one, "rev", [P, NT], F32)
        rev_chosen = sb(one, "rev_chosen", [P, TB, E], F32)
        slot_base = sb(one, "slot_base", [P, TB, E], F32)
        chosen_sum = sb(one, "chosen_sum", [P, E], F32)
        slot = sb(one, "slot", [P, TB, E], I32)
        slot_row = sb(one, "slot_row", [P, TB, E], I32)
        slot_col = sb(one, "slot_col", [P, TB, E], I32)
        row_hot = sb(one, "row_hot", [P, TB, E, P], FP16)
        col_hot = sb(one, "col_hot", [P, TB, E, LIST], FP16)
        iota_h = sb(one, "iota_h", [P, P], FP16)
        token_f = sb(one, "token_f", [P, NT], F32)
        top = sb(one, "top", [P, TB, 8], F32)
        shifted = sb(one, "shifted", [P, TB, E], F32)
        powers = sb(one, "powers", [P, TB, E], F32)
        total = sb(one, "total", [P, TB], F32)
        tri = sb(one, "tri", [P, P], BF16)
        ones = sb(one, "ones", [P, P], BF16)
        ps_xc = [ps(one, f"ps_xc{i}", [P, 2, D]) for i in range(2)]
        ps_wb = ps(one, "ps_wb", [P, 2, D])
        ps_rank = ps(one, "ps_rank", [P, TB + 1, E])
        ps_list = ps(one, "ps_list", [P, E, LIST])
        one.close()

        two = ExitStack()
        rows = [sb(two, f"rows{a}", [P, ROW], F32) for a in range(2)]
        g_hi = sb(two, "g_hi", [P, KC, SLOTS], F32R)
        g_lo = sb(two, "g_lo", [P, KC, SLOTS], F32R)
        b2_sb = sb(two, "b2_sb", [P, E, D], F32)
        hid = sb(two, "hid", [P, FC, SLOTS], F32)
        h_hi = sb(two, "h_hi", [P, FC, SLOTS], F32R)
        h_lo = sb(two, "h_lo", [P, FC, SLOTS], F32R)
        y_raw = [sb(two, f"y_raw{a}", [P, D], F32) for a in range(2)]
        y_out = [sb(two, f"y_out{a}", [P, D], F32) for a in range(2)]
        gate_table = sb(two, "gate_table", [P, E * LIST + 4, E], F32)
        gate_now = sb(two, "gate_now", [P, 2], F32)
        scatter_ix = [sb(two, f"scatter_ix{a}", [P, 1], I32) for a in range(2)]
        y_last = [sb(two, f"y_last{a}", [P, D], F32) for a in range(2)]
        last_scatter_ix = [sb(two, f"last_scatter_ix{a}", [P, 1], I32) for a in range(2)]
        ps_rows = ps(two, "ps_rows", [P, 2, KC, P])
        ps_hid = ps(two, "ps_hid", [P, FC, D])
        ps_y = ps(two, "ps_y", [P, 2, D])
        two.close()

        lora_in = sem("lora_in")
        small_in = sem("small_in")
        base_in = sem("base_in")
        bias_in = sem("bias_in")
        b1_in = sem("b1_in")
        router_in = sem("router_in")
        nat_in = sem("nat_in")
        base_nat_in = sem("base_nat_in")
        a_in = sem("a_in")
        x_loaded = [sem(f"x_loaded{i}") for i in range(2)]
        w_loaded = [sem(f"w_loaded{i}") for i in range(2)]
        out_init = sem("out_init")
        setup_step = sem("setup_step")
        a_split = sem("a_split")
        c_sum = sem("c_sum")
        c_root = sem("c_root")
        router_made = sem("router_made")
        router_kept = sem("router_kept")
        x_hi_done = sem("x_hi_done")
        x_lo_done = sem("x_lo_done")
        wb_done = sem("wb_done")
        wb_hi_done = sem("wb_hi_done")
        wb_lo_done = sem("wb_lo_done")
        lora_done = sem("lora_done")
        merged_done = sem("merged_done")
        merged_hi_done = sem("merged_hi_done")
        merged_lo_done = sem("merged_lo_done")
        merged_lo2_done = sem("merged_lo2_done")
        merged_used = sem("merged_used")
        linear_done = sem("linear_done")
        xc_done = sem("xc_done")
        xc_stored = [sem(f"xc_stored{i}") for i in range(2)]
        squares_done = sem("squares_done")
        norms_done = sem("norms_done")
        scores_kept = sem("scores_kept")
        route_step = sem("route_step")
        powers_done = sem("powers_done")
        gate_step = sem("gate_step")
        gates_stored = sem("gates_stored")
        mask_done = sem("mask_done")
        ranked = sem("ranked")
        chosen_summed = sem("chosen_summed")
        slot_step = sem("slot_step")
        row_hot_done = sem("row_hot_done")
        col_hot_done = sem("col_hot_done")
        listed = sem("listed")
        list_summed = sem("list_summed")
        w_hi_done = sem("w_hi_done")
        w_lo_done = sem("w_lo_done")

        tiles_step = sem("tiles_step")
        starts_step = sem("starts_step")
        b2_first_in = sem("b2_first_in")
        b2_in = sem("b2_in")
        first_hots = sem("first_hots")
        first_listed = sem("first_listed")
        lists_made = sem("lists_made")
        list_ready = sem("list_ready")
        ix_placed = sem("ix_placed")
        scatter_ix_done = sem("scatter_ix_done")
        gathered = [sem(f"gathered{a}") for a in range(2)]
        scattered = [sem(f"scattered{a}") for a in range(2)]
        rows_turned = sem("rows_turned")
        g_hi_done = sem("g_hi_done")
        g_lo_done = sem("g_lo_done")
        up_done = sem("up_done")
        gelu_done = sem("gelu_done")
        h_hi_done = sem("h_hi_done")
        h_lo_done = sem("h_lo_done")
        down_done = sem("down_done")
        y_biased = sem("y_biased")
        y_scaled = sem("y_scaled")

        LORA = 2 * 16
        SMALL = 3 * 16
        ROUTER = 3 * 16
        BASE_NAT = 2 * 16
        ROUTE, GATE, SLOT = 6, 4, 6

        block = ctx.enter_context(nc.Block())

        def over_batches(eng, batch):
            batch(0, 0, False)
            batch(1, 1, False)
            with eng.Fori(2, B - 1) as b:
                batch(b, 2, False)
            batch(B - 1, 2, True)

        def weigh(eng, b):
            wait(eng, lora_done, b * KC)
            wait(eng, wb_lo_done, b)
            eng.tensor_tensor(wb[:], b_sb[:], cond_sb[:, bass.ds(b, 1)].to_broadcast([P, WIDE]), ALU.mult)\
                .then_inc(wb_done, 1)

        def wb_low(eng, b):
            wait(eng, wb_hi_done, b + 1)
            eng.tensor_tensor(wb_lo[:], wb[:], wb_hi[:].bitcast(F32), ALU.subtract).then_inc(wb_lo_done, 1)

        def merged_low(eng, b, k):
            wait(eng, merged_hi_done, b * KC + k + 1)
            eng.tensor_tensor(merged_lo[:, k, :], merged[:, k, :], merged_hi[:, k, :].bitcast(F32), ALU.subtract)\
                .then_inc(merged_lo2_done if k == 2 else merged_lo_done, 1)

        def wait_merged_low(eng, b, k):
            if k == 2:
                wait(eng, merged_lo2_done, b + 1)
            else:
                wait(eng, merged_lo_done, b * (KC - 1) + (k + 1 if k < 2 else k))

        def router_base_at(c):
            return (ps_xc[1][:, 0, 0:E2], ps_xc[1][:, 1, 0:E2], ps_list[:, 0, 0:E2],
                    ps_rank[:, 0:2, :].rearrange("p a e -> p (a e)"))[c]

        def halves(wide):
            return wide.rearrange("p (h c) -> p h c", h=2)

        def over_tiles(eng, stage, started):
            eng.wait_ge(starts_step, started)
            first = 0
            for e in range(E):
                last = eng.value_load(starts[0:1, e + 1:e + 2], min_val=0, max_val=LIST // 2 * (e + 1) - 2) + 2
                stage(first, e, e - 1)
                with eng.Fori(first + 1, last) as g:
                    stage(g, e, e)
                first = last
            return first

        @block.sync
        def _(sp):
            def load(dst, src, semaphore):
                sp.dma_start(dst, src).then_inc(semaphore, 16)

            def x_tile(n):
                return xT[bass.ds(n * P, P), :].rearrange("p (k t) -> p k t", k=KC)

            def load_weights(b, half):
                wait(sp, w_hi_done, (b - 1) * TB + 2 * half + 2)
                at = bass.ds((b * TB + 2 * half) * WCH, 2 * WCH)
                sp.dma_start(w_raw[:, at], weights[:, at]).then_inc(w_loaded[half], 16)

            chunks = "p (k o) -> p k o"
            load(router[0:E, :], centroids, router_in)
            load(router[E:E2, :], w_route, router_in)
            load(ident[:], consts[:, IDENT:IDENT + P], router_in)
            load(b_nat[:], lora_bT.rearrange(chunks, k=KC), nat_in)
            load(b_sb[:, 0:D], lora_b, lora_in)
            load(cond_sb[:, 0:B], cond, lora_in)
            load(a_raw[:], lora_a, a_in)
            load(base_nat[:], base_w.rearrange(chunks, k=KC), base_nat_in)
            load(bias_col[:], base_bT, base_nat_in)
            load(base_sb[:, :, 0:D], base_wT.rearrange(chunks, k=KC), base_in)
            load(x_in[0][:], x_tile(0), x_loaded[0])
            load(bias[:, 0:D], base_b.partition_broadcast(P), bias_in)
            load(x_in[1][:], x_tile(1), x_loaded[1])
            load_weights(0, 0)
            load(iota_f[:], consts[:, IOTA:IOTA + P], small_in)
            load(tri_f[:], consts[:, TRI:TRI + P], small_in)
            load(token_f[:], consts[:, TOKEN:TOKEN + NT], small_in)
            load(b1_sb[:], b1, b1_in)
            sp.sem_inc(gates_stored, 16)
            sp.wait_ge(x_lo_done, 1)
            load(x_in[0][:], x_tile(2), x_loaded[0])

            def batch(b, before, last):
                for t in range(TB):
                    n = b * TB + t
                    if not (last and t >= TB - 3):
                        wait(sp, x_lo_done, n + 2)
                        load(x_in[(t + 3) % 2][:], x_tile(n + 3), x_loaded[(t + 3) % 2])
                    if not (last and t >= TB - 2):
                        sp.dma_start(out[bass.ds(n * P, P), :], x[bass.ds(n * P, P), :]).then_inc(out_init, 16)
                    wait(sp, xc_done, n + 1)
                    sp.dma_start(xc_rows[bass.ds(n * P, P), 0:D], xc[t % 2][:, 0:D]).then_inc(xc_stored[t % 2], 16)
                    if t == 0:
                        load_weights(b, 1)
                    if t == 2 and not last:
                        load_weights(b + 1, 0)
                    if t == 3 and before:
                        store_gates(b - 1)

            def store_gates(b):
                wait(sp, gate_step, (b + 1) * GATE)
                sp.dma_start(xc_tiles[:, bass.ds(b * TB, TB), D:ROW], gates[:]).then_inc(gates_stored, 16)

            over_batches(sp, batch)
            sp.wait_ge(linear_done, NT)
            load(b2_sb[:, 0, :], b2[0].partition_broadcast(P), b2_first_in)
            store_gates(B - 1)
            for e in range(1, E):
                sp.wait_ge(gathered[1], 16 * e)
                if e > 1:
                    sp.wait_ge(b2_in, 16 * (e - 1))
                load(b2_sb[:, e, :], b2[e].partition_broadcast(P), b2_in)

        @block.gpsimd
        def _(pool):
            def x_low(n, t):
                wait(pool, x_hi_done, n + 1)
                pool.tensor_tensor(x_lo[t % 2][:], x_in[t % 2][:], x_hi[t % 2][:].bitcast(F32), ALU.subtract)\
                    .then_inc(x_lo_done, 1)

            def root(b):
                wait(pool, squares_done, TB * (b + 1))
                wait(pool, route_step, (b - 1) * ROUTE + 1 if not isinstance(b, int) or b else 0)
                pool.tensor_tensor(norms[:], sumsq[:], half[:], ALU.pow).then_inc(norms_done, 1)

            def rev_of_chosen(b):
                wait(pool, slot_step, b * SLOT)
                wait_before(pool, (small_in, SMALL), mask_done, b + 1)
                later = rev[:, bass.ds(b * TB, TB)].unsqueeze(2).to_broadcast([P, TB, E])
                pool.tensor_tensor(rev_chosen[:], later, mask[:, 0:TB, :], ALU.mult)\
                    .then_inc(slot_step, 1)

            def rev_of_others(b):
                wait_before(pool, (small_in, SMALL), slot_step, b * SLOT + 1)
                later = rev[:, bass.ds(b * TB, TB)].unsqueeze(2).to_broadcast([P, TB, E])
                pool.tensor_tensor(slot_base[:], later, rev_chosen[:], ALU.subtract)\
                    .then_inc(slot_step, 1)

            def add_chosen_before(b):
                wait(pool, slot_step, b * SLOT + 2)
                wait(pool, chosen_summed, b)
                pool.tensor_tensor(slot_base[:], slot_base[:], chosen_sum[:].unsqueeze(1).to_broadcast([P, TB, E]), ALU.add)\
                    .then_inc(slot_step, 1)

            def base_slots(b):
                rev_of_chosen(b)
                rev_of_others(b)
                add_chosen_before(b)

            def weights_low(n):
                wait(pool, w_hi_done, n + 1)
                at = bass.ds(n * WCH, WCH)
                pool.tensor_tensor(w_lo[:, at], w_raw[:, at], w_hi[:, at].bitcast(F32), ALU.subtract)\
                    .then_inc(w_lo_done, 1)

            x_low(0, 0)
            weigh(pool, 1)
            wb_low(pool, 1)

            def batch(b, before, last):
                for t in range(TB):
                    n = b * TB + t
                    if t == TB - 1 and not last:
                        weigh(pool, b + 2)
                    if not (last and t == TB - 1):
                        x_low(n + 1, t + 1)
                    if t == TB - 1 and not last:
                        merged_low(pool, b + 1, 2)
                        wb_low(pool, b + 2)
                    if t == 0 and before:
                        root(b - 1)
                    if before and t < 2 or t == 2:
                        weights_low(n - 2)
                    if t == 1 and before:
                        base_slots(b - 1)
                    if t == 2:
                        weights_low(n - 1)
                    if t < 2 and last:
                        at = slice((NT - 2 + t) * P, (NT - 1 + t) * P)
                        pool.dma_start(out[at, :], x[at, :]).then_inc(scattered[t], 16)

            over_batches(pool, batch)
            root(B - 1)
            base_slots(B - 1)
            weights_low(NT - 2)
            weights_low(NT - 1)

            pool.wait_ge(tiles_step, 3)
            pool.memset(starts[:, 0:1], -2).then_inc(starts_step, 1)
            for e in range(E):
                pool.wait_ge(starts_step, e + 1)
                pool.tensor_tensor(starts[:, e + 1:e + 2], starts[:, e:e + 1], tiles_i[:, e:e + 1], ALU.add)\
                    .then_inc(starts_step, 1)

            def gather(g, a):
                wait(pool, rows_turned, 2 * g + a - 1)
                wait_before(pool, (list_ready, 1), ix_placed, 2 * g + a + 1)
                pool.indirect_dma_start(rows[a][:], None, xc_rows,
                                        bass.IndirectOffsetOnAxis(ap=gather_ix[a][:, 0:1], axis=0))\
                    .then_inc(gathered[a], 16)

            def place_scatter_ix(g, a, ix=scatter_ix):
                pool.tensor_copy(ix[a][:], lists[:, bass.ds(2 * g + a, 1)]).then_inc(scatter_ix_done, 1)

            def scatter(g, a, ix=scatter_ix, y=y_out):
                pool.wait_ge(scatter_ix_done, 2 * g + 2)
                wait_before(pool, (list_ready, 1), y_scaled, 2 * g + a + 3)
                pool.indirect_dma_start(out, bass.IndirectOffsetOnAxis(ap=ix[a][:, 0:1], axis=0),
                                        y[a][:], None, compute_op=ALU.add).then_inc(scattered[a], 16)

            def scattered_before(g):
                for a in range(2):
                    pool.wait_ge(scattered[a], 16 * (g + 1))

            for i in range(2):
                pool.wait_ge(xc_stored[i], 16 * (NT // 2))
            pool.wait_ge(gates_stored, 16 * (B + 1))
            pool.wait_ge(out_init, 16 * (NT - 2))
            for a in range(2):
                gather(0, a)
            list_starts = [pool.value_load(starts[0:1, e:e + 1], min_val=0, max_val=LIST // 2 * e) + 2 for e in range(1, E)]
            for a in range(2):
                gather(1, a)
            pool.wait_ge(lists_made, 1)
            for e in range(1, E):
                pool.wait_ge(list_ready, e)
                pool.tensor_copy(lists[:, bass.ds(2 * list_starts[e - 1], LIST)], lists_apart[:, e, :])\
                    .then_inc(list_ready, 1)

            def stage(g, e, e_before):
                for a in range(2):
                    gather(g + 2, a)
                if not isinstance(g, int):
                    scattered_before(g - 1)
                    for a in range(2):
                        place_scatter_ix(g - 1, a)
                    for a in range(2):
                        scatter(g - 1, a)

            g = over_tiles(pool, stage, E + 1)
            for a in range(2):
                place_scatter_ix(g - 1, a, last_scatter_ix)
            for a in range(2):
                scatter(g - 1, a, last_scatter_ix, y_last)
            scattered_before(g)
            for a in range(2):
                pool.wait_ge(gathered[a], 16 * (g + 2))

        @block.scalar
        def _(act):
            act.wait_ge(setup_step, 1)
            act.activation(c_norm[:, 1:2], c_norm[:, 0:1], ACT.Sqrt).then_inc(c_sum, 1)
            act.wait_ge(router_in, ROUTER)
            act.wait_ge(c_sum, 1)
            act.activation(squares[0:E, :], router[0:E, :], ACT.Square, accum_out=c_norm[:, 0:1]).then_inc(c_sum, 1)
            act.wait_ge(c_sum, 2)
            act.activation(c_norm[:, 1:2], c_norm[:, 0:1], ACT.Sqrt).then_inc(c_root, 1)
            act.wait_ge(a_in, 16)
            act.activation(a_hi[:], a_raw[:], ACT.Copy).then_inc(a_split, 1)

            def x_high(n, t):
                wait(act, x_loaded[t % 2], (n // 2 + 1) * 16 if isinstance(n, int) else (n - t) * 8 + (t // 2 + 1) * 16)
                wait(act, linear_done, n - 1)
                act.activation(x_hi[t % 2][:], x_in[t % 2][:], ACT.Copy).then_inc(x_hi_done, 1)

            def wb_high(b):
                wait(act, wb_done, b + 1)
                act.activation(wb_hi[:], wb[:], ACT.Copy).then_inc(wb_hi_done, 1)

            def merged_high(b, k):
                wait(act, merged_done, b * KC + k + 1)
                if k < KC - 1:
                    wait(act, merged_used, (b - 1) * (KC - 1) + k + 1)
                else:
                    wait(act, linear_done, b * TB)
                act.activation(merged_hi[:, k, :], merged[:, k, :], ACT.Copy).then_inc(merged_hi_done, 1)

            def weights_high(n, t, b):
                wait(act, w_loaded[t // 2], b * 16 + 16)
                at = bass.ds(n * WCH, WCH)
                act.activation(w_hi[:, at], w_raw[:, at], ACT.Copy).then_inc(w_hi_done, 1)

            def square(n, t, b):
                wait(act, xc_done, n + 1)
                wait(act, squares_done, n)
                if t == 0:
                    wait(act, norms_done, b)
                act.activation(squares[:], xc[t % 2][:, 0:D], ACT.Square, accum_out=sumsq[:, t:t + 1])\
                    .then_inc(squares_done, 1)

            def keep_scores(n, t):
                wait(act, xc_done, n + 1)
                act.activation(scores[:, t, :], xc[t % 2][:, D:WIDE], ACT.Copy).then_inc(scores_kept, 1)

            def after_linear(n, t, b, batch_before):
                square(n, t, b)
                if t:
                    keep_scores(n, t)
                weights_high(n, t, b - 1 if batch_before else b)

            def power(b):
                wait(act, route_step, b * ROUTE + 6)
                act.activation(powers[:], shifted[:], ACT.Exp).then_inc(powers_done, 1)

            wb_high(0)
            x_high(0, 0)
            for k in range(KC):
                merged_high(0, k)

            wb_high(1)

            def col_times_token(b, t, experts=slice(0, E)):
                wait(act, col_hot_done, b * (TB + 1) + 1)
                act.activation(col_hot[:, t, experts, :], col_hot[:, t, experts, :], ACT.Identity,
                               scale=token_f[:, bass.ds(b * TB + t, 1)]).then_inc(col_hot_done, 1)

            def batch(b, before, last):
                for t in range(TB):
                    n = b * TB + t
                    if t == TB - 1 and last:
                        for i in range(TB):
                            col_times_token(b - 1, i)
                    if not (last and t == TB - 1):
                        x_high(n + 1, t + 1)
                    if t == TB - 1 and not last:
                        for k in range(KC):
                            merged_high(b + 1, k)
                        wb_high(b + 2)
                    if t == 0 and before:
                        after_linear(n - 2, TB - 2, b, True)
                    if (t or before) and (t < TB - 1 or last):
                        after_linear(n - 1, (t - 1) % TB, b, t == 0)
                    if t == 1 and before == 2:
                        for i in range(TB):
                            col_times_token(b - 2, i)
                    if t == 1 and before:
                        power(b - 1)
                    if t == 1:
                        keep_scores(n - 1, 0)

            over_batches(act, batch)
            square(NT - 1, TB - 1, B - 1)
            keep_scores(NT - 1, TB - 1)
            power(B - 1)
            weights_high(NT - 1, TB - 1, B - 1)
            for t in range(TB):
                col_times_token(B - 1, t, slice(1, E))

            def gelu(g, f, e):
                wait(act, up_done, 2 * g + f + 1)
                wait(act, h_lo_done, 2 * g)
                act.activation(hid[:, f, :], ps_hid[:, f, 0:SLOTS], ACT.Gelu, bias=b1_sb[:, e * FC + f:e * FC + f + 1])\
                    .then_inc(gelu_done, 1)

            def gathered_high(g, a):
                wait(act, rows_turned, 2 * g + a + 1)
                wait(act, up_done, 2 * g)
                act.activation(g_hi[:, :, a * P:(a + 1) * P], ps_rows[:, a, :, :], ACT.Copy).then_inc(g_hi_done, 1)

            def hidden_high(g, a):
                wait(act, gelu_done, 2 * g + 2)
                wait(act, down_done, 2 * g - 1 + a if not isinstance(g, int) else (2 * g - 1 + a if g else 0))
                act.activation(h_hi[:, :, a * P:(a + 1) * P], hid[:, :, a * P:(a + 1) * P], ACT.Copy)\
                    .then_inc(h_hi_done, 1)

            def scale(g, a):
                act.wait_ge(y_biased, 2 * g + a + 3)
                act.wait_ge(scattered[a], 16 * (g + 1))
                act.activation(y_out[a][:], y_raw[a][:], ACT.Identity, scale=gate_now[:, a:a + 1])\
                    .then_inc(y_scaled, 1)

            act.wait_ge(b1_in, 16)
            act.sem_inc(y_scaled, 2)
            for a in range(2):
                gathered_high(0, a)

            def stage(g, e, e_before):
                for f in range(FC):
                    gelu(g, f, e)
                for a in range(2):
                    gathered_high(g + 1, a)
                for a in range(2):
                    hidden_high(g, a)
                    if not isinstance(g, int):
                        scale(g - 1, a)

            g = over_tiles(act, stage, E + 1)
            for a in range(2):
                act.wait_ge(y_biased, 2 * (g - 1) + a + 3)
                act.activation(y_last[a][:], y_raw[a][:], ACT.Identity, scale=gate_now[:, a:a + 1]).then_inc(y_scaled, 1)

        @block.vector
        def _(vec):
            def stepper(semaphore, start):
                count = [0]

                def step(instruction):
                    instruction.then_inc(semaphore, 1)
                    count[0] += 1
                    vec.wait_ge(semaphore, start + count[0])
                return step

            step = stepper(setup_step, 0)
            step(vec.memset(c_norm[:], 0.0))
            step(vec.memset(cond_sb[:, B:B + 1], 0.0))
            step(vec.memset(half[:], 0.5))
            step(vec.memset(ones[:], 1.0))
            step(vec.memset(mask[:, TB, :], 0.0))
            step(vec.memset(chosen_sum[:], 0.0))
            step(vec.memset(list_sums[:], 0.0))
            step(vec.memset(lists[:], 0))

            def merge(b, k):
                wait(vec, lora_done, b * KC + k + 1)
                if not isinstance(b, int) or b:
                    wait_merged_low(vec, b - 1, k)
                vec.tensor_tensor(halves(merged[:, k, :]), ps_wb[:, :, 0:HALF], halves(base_sb[:, k, :]), ALU.add)\
                    .then_inc(merged_done, 1)

            def linear_out(n, t):
                wait(vec, linear_done, n + 1)
                wait(vec, squares_done, n - 1)
                wait(vec, scores_kept, n - 1)
                wait(vec, xc_stored[t % 2], n // 2 * 16 if isinstance(n, int) else (n - t) * 8 + t // 2 * 16)
                vec.tensor_tensor(halves(xc[t % 2][:]), ps_xc[t % 2][:, :, 0:HALF], halves(bias[:]), ALU.add)\
                    .then_inc(xc_done, 1)

            def wide(column):
                return column.unsqueeze(2).to_broadcast([P, TB, E])

            def norm(b):
                wait(vec, route_step, b * ROUTE)
                wait(vec, norms_done, b + 1)
                vec.tensor_scalar(inv_norm[:], norms[:], NORM_EPS, None, ALU.max).then_inc(route_step, 1)

            def invert_norm(b):
                wait(vec, route_step, b * ROUTE + 1)
                vec.reciprocal(inv_norm[:], inv_norm[:]).then_inc(route_step, 1)

            def cosines(b):
                wait(vec, route_step, b * ROUTE + 2)
                wait(vec, scores_kept, TB * (b + 1))
                vec.tensor_tensor(logits[:], scores[:, :, 0:E], wide(inv_norm[:]), ALU.mult).then_inc(route_step, 1)

            def add_route_scores(b):
                wait(vec, route_step, b * ROUTE + 3)
                vec.tensor_tensor(logits[:], logits[:], scores[:, :, E:E2], ALU.add).then_inc(route_step, 1)

            def find_top(b):
                wait_before(vec, (small_in, SMALL), route_step, b * ROUTE + 4)
                for t in range(TB):
                    last = vec.max(top[:, t, :], logits[:, t, :])
                last.then_inc(route_step, 1)

            def choose(b):
                wait(vec, route_step, b * ROUTE + 5)
                wait(vec, ranked, b)
                vec.tensor_tensor(mask[:, 0:TB, :], logits[:], top[:, :, 1:2].to_broadcast([P, TB, E]), ALU.is_ge)\
                    .then_inc(mask_done, 1)

            def less_maximum(b):
                vec.tensor_tensor(shifted[:], logits[:], top[:, :, 0:1].to_broadcast([P, TB, E]), ALU.subtract)\
                    .then_inc(route_step, 1)

            def chosen_powers(b):
                wait(vec, gate_step, b * GATE)
                wait(vec, powers_done, b + 1)
                vec.tensor_tensor(powers[:], powers[:], mask[:, 0:TB, :], ALU.mult).then_inc(gate_step, 1)

            def total_power(b):
                wait(vec, gate_step, b * GATE + 1)
                vec.tensor_reduce(total[:], powers[:], AX_X, ALU.add).then_inc(gate_step, 1)

            def invert_total(b):
                wait(vec, gate_step, b * GATE + 2)
                vec.reciprocal(total[:], total[:]).then_inc(gate_step, 1)

            def gate(b):
                wait(vec, gate_step, b * GATE + 3)
                wait(vec, gates_stored, 16 * (b + 1))
                vec.tensor_tensor(gates[:], powers[:], wide(total[:]), ALU.mult).then_inc(gate_step, 1)

            def slots(b):
                wait(vec, slot_step, b * SLOT + 3)
                wait(vec, ranked, b + 1)
                wait(vec, row_hot_done, b * TB)
                vec.tensor_tensor(slot[:], ps_rank[:, 0:TB, :], slot_base[:], ALU.add).then_inc(slot_step, 1)

            def sum_chosen(b):
                vec.tensor_tensor(chosen_sum[:], chosen_sum[:], ps_rank[:, TB, :], ALU.add).then_inc(chosen_summed, 1)

            def slot_rows(b):
                wait(vec, slot_step, b * SLOT + 4)
                vec.tensor_scalar(slot_row[:], slot[:], P - 1, None, ALU.bitwise_and).then_inc(slot_step, 1)

            def slot_cols(b):
                vec.tensor_scalar(slot_col[:], slot[:], P.bit_length() - 1, None, ALU.logical_shift_right)\
                    .then_inc(slot_step, 1)

            def row_one_hot(b, t, experts=slice(0, E)):
                wait(vec, slot_step, b * SLOT + 6)
                shape = [P, experts.stop - experts.start, P]
                vec.tensor_tensor(row_hot[:, t, experts, :], iota_h[:].unsqueeze(1).to_broadcast(shape),
                                  slot_row[:, t, experts].unsqueeze(2).to_broadcast(shape), ALU.is_equal)\
                    .then_inc(row_hot_done, 1)

            def col_one_hot(b, experts=slice(0, E)):
                wait(vec, slot_step, b * SLOT + 6)
                wait(vec, listed, b)
                shape = [P, TB, experts.stop - experts.start, LIST]
                vec.tensor_tensor(col_hot[:, :, experts, :], iota_h[:, 0:LIST].unsqueeze(1).unsqueeze(1).to_broadcast(shape),
                                  slot_col[:, :, experts].unsqueeze(3).to_broadcast(shape), ALU.is_equal)\
                    .then_inc(col_hot_done, 1)

            def sum_lists(b):
                wait(vec, listed, b + 1)
                wait(vec, list_summed, b + 1)
                vec.tensor_tensor(list_sums[:], list_sums[:], ps_list[:], ALU.add).then_inc(list_summed, 1)

            vec.sem_inc(list_summed, 1)
            vec.wait_ge(lora_in, LORA)
            step(vec.tensor_scalar(cond_sb[:, 0:B], cond_sb[:, 0:B], SCALING, None, ALU.mult))
            vec.wait_ge(c_root, 1)
            step(vec.tensor_scalar(c_norm[:, 2:3], c_norm[:, 1:2], NORM_EPS, None, ALU.max))
            step(vec.reciprocal(c_norm[:, 3:4], c_norm[:, 2:3]))
            step(vec.tensor_scalar(router[0:E, :], router[0:E, :], c_norm[:, 3:4], None, ALU.mult))
            vec.wait_ge(router_made, 1)
            vec.tensor_copy(routerT[:], ps_list[:, 0:2, :].rearrange("p a c -> p (a c)")
                            .rearrange("p (k e) -> p k e", k=KC)).then_inc(router_kept, 1)
            vec.wait_ge(a_split, 1)
            step(vec.tensor_tensor(a_lo[:], a_raw[:], a_hi[:].bitcast(F32), ALU.subtract))
            vec.wait_ge(router_made, 2)
            vec.tensor_copy(b_sb[:, D:WIDE], ps_xc[0][:, 0, 0:E2]).then_inc(router_kept, 1)
            vec.wait_ge(router_kept, 2)
            weigh(vec, 0)
            wb_low(vec, 0)
            vec.wait_ge(base_nat_in, BASE_NAT)
            step(vec.tensor_copy(bias_nat[:], bias_col[:].unsqueeze(2).to_broadcast([P, KC, P])))
            vec.wait_ge(base_in, 16)
            for k in range(KC):
                vec.wait_ge(router_made, 3 + k)
                vec.tensor_copy(base_sb[:, k, D:WIDE], router_base_at(k)).then_inc(router_kept, 1)
                vec.wait_ge(router_kept, 3 + k)
                merge(0, k)
                if k:
                    merged_low(vec, 0, k - 1)
            merged_low(vec, 0, KC - 1)
            vec.wait_ge(router_made, 3 + KC)
            vec.tensor_copy(bias[:, D:WIDE], ps_xc[1][:, 0, 0:E2]).then_inc(router_kept, 1)
            vec.wait_ge(router_kept, 3 + KC)
            vec.wait_ge(small_in, SMALL)
            step(vec.tensor_copy(tri[:], tri_f[:]))
            step(vec.tensor_copy(iota_h[:], iota_f[:]))
            step(vec.tensor_scalar(rev[:], token_f[:], -1.0, float(T // 2 - 1), ALU.mult, ALU.add))
            vec.wait_ge(bias_in, 16)

            def batch(b, before, last):
                if before == 2:
                    row_one_hot(b - 2, 0)
                    row_one_hot(b - 2, 1)
                linear_out(b * TB, 0)
                if before:
                    norm(b - 1)
                if not last:
                    merge(b + 1, 0)
                if before:
                    invert_norm(b - 1)
                if before:
                    cosines(b - 1)
                    add_route_scores(b - 1)
                    find_top(b - 1)
                    choose(b - 1)
                    less_maximum(b - 1)
                if before == 2:
                    row_one_hot(b - 2, 2)
                if not last:
                    merge(b + 1, 1)
                if before == 2:
                    row_one_hot(b - 2, 3)
                linear_out(b * TB + 1, 1)
                if not last:
                    merge(b + 1, 2)
                if before:
                    chosen_powers(b - 1)
                    slots(b - 1)
                    total_power(b - 1)
                    sum_chosen(b - 1)
                    slot_rows(b - 1)
                    invert_total(b - 1)
                    slot_cols(b - 1)
                    gate(b - 1)
                if before == 2:
                    sum_lists(b - 2)
                if not last:
                    linear_out(b * TB + 2, 2)
                    merge(b + 1, 3)
                if before:
                    col_one_hot(b - 1)
                if not last:
                    merged_low(vec, b + 1, 0)
                    merged_low(vec, b + 1, 1)
                    merged_low(vec, b + 1, 3)
                    linear_out(b * TB + 3, 3)
                if last:
                    row_one_hot(b - 1, 0)
                    linear_out(b * TB + 2, 2)
                    linear_out(b * TB + 3, 3)

            over_batches(vec, batch)
            row_one_hot(B - 2, 1)
            row_one_hot(B - 2, 2)
            norm(B - 1)
            invert_norm(B - 1)
            cosines(B - 1)
            add_route_scores(B - 1)
            find_top(B - 1)
            choose(B - 1)
            less_maximum(B - 1)
            row_one_hot(B - 2, 3)
            chosen_powers(B - 1)
            slots(B - 1)
            total_power(B - 1)
            sum_chosen(B - 1)
            slot_rows(B - 1)
            invert_total(B - 1)
            slot_cols(B - 1)
            gate(B - 1)
            vec.wait_ge(chosen_summed, B)
            step = stepper(tiles_step, 0)
            step(vec.tensor_scalar(tiles_i[:], chosen_sum[:], float(SLOTS - 1), None, ALU.add))
            step(vec.tensor_scalar(tiles_i[:], tiles_i[:], SLOTS.bit_length() - 1, None, ALU.logical_shift_right))
            step(vec.tensor_scalar(tiles_i[:], tiles_i[:], 2.0, None, ALU.max))

            sum_lists(B - 2)
            now = slice((B - 1) * TB, B * TB)
            shape = [P, TB, LIST]
            vec.wait_ge(slot_step, B * SLOT)
            step = stepper(first_hots, 0)
            step(vec.tensor_tensor(col_hot[:, :, 0, :], iota_h[:, 0:LIST].unsqueeze(1).to_broadcast(shape),
                                   slot_col[:, :, 0].unsqueeze(2).to_broadcast(shape), ALU.is_equal))
            step(vec.tensor_tensor(col_hot[:, :, 0, :], col_hot[:, :, 0, :],
                                   token_f[:, now].unsqueeze(2).to_broadcast(shape), ALU.mult))
            shape = [P, TB, P]
            step(vec.tensor_tensor(row_hot[:, :, 0, :], iota_h[:].unsqueeze(1).to_broadcast(shape),
                                   slot_row[:, :, 0].unsqueeze(2).to_broadcast(shape), ALU.is_equal))
            vec.wait_ge(first_listed, 1)
            vec.tensor_tensor(list_sums[:, 0, :], list_sums[:, 0, :], ps_list[:, 0, :], ALU.add).then_inc(list_summed, 1)
            vec.wait_ge(list_summed, B + 1)
            vec.tensor_scalar(lists[:, 0:LIST], list_sums[:, 0, :], float(T // 2), None, ALU.add).then_inc(list_ready, 1)
            vec.wait_ge(list_ready, 1)
            for a in range(2):
                vec.tensor_copy(gather_ix[a][:], lists[:, a:a + 1]).then_inc(ix_placed, 1)
            others = slice(1, E)
            col_one_hot(B - 1, others)
            for t in range(TB):
                row_one_hot(B - 1, t, others)

            def keep_gates(g, a):
                vec.wait_ge(gathered[a], 16 * (g + 1))
                vec.tensor_copy(gate_table[:, bass.ds(2 * g + a, 1), :], rows[a][:, D:ROW].unsqueeze(1))
                vec.tensor_copy(gather_ix[a][:], lists[:, bass.ds(2 * g + 2 + a, 1)]).then_inc(ix_placed, 1)

            def gathered_low(g, a):
                wait(vec, g_hi_done, 2 * g + a + 1)
                vec.tensor_tensor(g_lo[:, :, a * P:(a + 1) * P], ps_rows[:, a, :, :],
                                  g_hi[:, :, a * P:(a + 1) * P].bitcast(F32), ALU.subtract).then_inc(g_lo_done, 1)

            def hidden_low(g, a):
                wait(vec, h_hi_done, 2 * g + a + 1)
                cols = slice(a * P, (a + 1) * P)
                vec.tensor_tensor(h_lo[:, :, cols], hid[:, :, cols], h_hi[:, :, cols].bitcast(F32), ALU.subtract)\
                    .then_inc(h_lo_done, 1)

            def add_bias(g, a, e):
                vec.wait_ge(y_scaled, 2 * g + a + 1)
                vec.tensor_copy(gate_now[:, a:a + 1], gate_table[:, bass.ds(2 * g + a, 1), e])
                vec.wait_ge(down_done, 2 * g + a + 1)
                vec.tensor_tensor(y_raw[a][:], ps_y[:, a, :], b2_sb[:, e, :], ALU.add).then_inc(y_biased, 1)

            vec.sem_inc(y_biased, 2)
            for a in range(2):
                keep_gates(0, a)
            for a in range(2):
                gathered_low(0, a)
            vec.wait_ge(listed, B)
            vec.tensor_tensor(list_sums[:, others, :], list_sums[:, others, :], ps_list[:, others, :], ALU.add)\
                .then_inc(list_summed, 1)
            vec.wait_ge(list_summed, B + 2)
            vec.tensor_scalar(lists_apart[:], list_sums[:], float(T // 2), None, ALU.add).then_inc(lists_made, 1)
            vec.wait_ge(b2_first_in, 16)
            vec.wait_ge(list_ready, E)

            def stage(g, e, e_before):
                if e and e_before < e:
                    vec.wait_ge(b2_in, 16 * e)
                for a in range(2):
                    keep_gates(g + 1, a)
                for a in range(2):
                    gathered_low(g + 1, a)
                for a in range(2):
                    if not isinstance(g, int):
                        add_bias(g - 1, a, e_before)
                    hidden_low(g, a)

            g = over_tiles(vec, stage, E + 1)
            for a in range(2):
                add_bias(g - 1, a, E - 1)

        @block.tensor
        def _(pe):
            def split_product(dst, sta, mov, start, stop):
                pe.matmul(dst, sta[0], mov[0], start=start, stop=False)
                pe.matmul(dst, sta[0], mov[1], start=False, stop=False)
                return pe.matmul(dst, sta[1], mov[0], start=False, stop=stop)

            def wide_product(dst, sta, mov, start, stop):
                for i, (s, m) in enumerate(((0, 0), (0, 1), (1, 0))):
                    for h in range(2):
                        last = pe.matmul(dst[:, h, 0:HALF], sta[s], mov[m][:, h * HALF:(h + 1) * HALF],
                                         start=start and i == 0, stop=stop and i == 2)
                return last

            def adapters(b, k):
                if k == 0:
                    wait(pe, wb_lo_done, b + 1)
                wait(pe, merged_done, b * KC + k)
                cols = slice(k * P, (k + 1) * P)
                wide_product(ps_wb, (a_hi[:, cols], a_lo[:, cols]), (wb_hi, wb_lo), True, True)\
                    .then_inc(lora_done, 1)

            def linear(n, b, t, last_batch):
                wait(pe, x_lo_done, n + 1)
                wait(pe, xc_done, n - 1)
                for k in range(KC):
                    if t == 0:
                        wait_merged_low(pe, b, k)
                    if t == 2 and k == 2 and not last_batch:
                        adapters(b + 1, 2)
                    last = wide_product(ps_xc[t % 2], (x_hi[t % 2][:, k, :], x_lo[t % 2][:, k, :]),
                                        (merged_hi[:, k, :], merged_lo[:, k, :]), k == 0, k == KC - 1)
                    if t == TB - 1 and k < KC - 1:
                        last.then_inc(merged_used, 1)
                last.then_inc(linear_done, 1)

            def rank_tokens(b):
                wait(pe, mask_done, b + 1)
                wait(pe, chosen_summed, b)
                pe.matmul(ps_rank[:], tri[:], mask[:], start=True, stop=False)
                for i in range(1, TB + 1):
                    last = pe.matmul(ps_rank[:, i:TB + 1, :], ones[:], mask[:, 0:TB + 1 - i, :],
                                     start=False, stop=(i == TB))
                last.then_inc(ranked, 1)

            def make_lists(b, experts=range(E)):
                wait(pe, row_hot_done, (b + 1) * TB)
                wait(pe, col_hot_done, (b + 1) * (TB + 1))
                wait(pe, list_summed, b + 1)
                for e in experts:
                    for t in range(TB):
                        last = pe.matmul(ps_list[:, e, :], row_hot[:, t, e, :], col_hot[:, t, e, :],
                                         start=(t == 0), stop=(t == TB - 1))
                last.then_inc(listed, 1)

            pe.wait_ge(setup_step, 12)
            turned = ps_list[:, 0:2, :].rearrange("p a c -> p (a c)")
            for k in range(KC):
                last = pe.transpose(turned[:, k * E2:(k + 1) * E2], router[:, k * P:(k + 1) * P], ident[0:E2, 0:E2])
            last.then_inc(router_made, 1)
            pe.wait_ge(router_kept, 1)
            pe.wait_ge(nat_in, 16)
            for k in range(KC):
                last = pe.matmul(ps_xc[0][:, 0, 0:E2], b_nat[:, k, :], routerT[:, k, :], start=(k == 0), stop=(k == KC - 1))
            last.then_inc(router_made, 1)
            pe.wait_ge(base_nat_in, BASE_NAT)

            def base_rows(c):
                for k in range(KC):
                    last = pe.matmul(router_base_at(c), base_nat[:, k, c * P:(c + 1) * P], routerT[:, k, :],
                                     start=(k == 0), stop=(k == KC - 1))
                last.then_inc(router_made, 1)

            base_rows(0)
            pe.wait_ge(setup_step, 13)
            for c in range(1, KC):
                base_rows(c)
                adapters(0, c - 1)
            pe.wait_ge(setup_step, 14)
            for k in range(KC):
                last = pe.matmul(ps_xc[1][:, 0, 0:E2], bias_nat[:, k, :], routerT[:, k, :], start=(k == 0), stop=(k == KC - 1))
            last.then_inc(router_made, 1)
            adapters(0, KC - 1)

            def batch(b, before, last):
                for t in range(TB):
                    n = b * TB + t
                    if t == 1 and not before:
                        pe.wait_ge(router_kept, 3 + KC)
                    linear(n, b, t, last)
                    if t < 2 and not last:
                        adapters(b + 1, t)
                    if t == 2 and before == 2:
                        make_lists(b - 2)
                    if t == 2 and not last:
                        adapters(b + 1, 3)
                    if t == 1 and before:
                        rank_tokens(b - 1)

            over_batches(pe, batch)
            rank_tokens(B - 1)
            make_lists(B - 2)
            pe.wait_ge(first_hots, 3)
            pe.wait_ge(list_summed, B)
            for t in range(TB):
                last = pe.matmul(ps_list[:, 0, :], row_hot[:, t, 0, :], col_hot[:, t, 0, :], start=(t == 0), stop=(t == TB - 1))
            last.then_inc(first_listed, 1)
            pe.wait_ge(list_summed, B + 1)

            def turn_rows(g, a):
                pe.wait_ge(gathered[a], 16 * (g + 1))
                wait(pe, g_lo_done, 2 * g + a - 1)
                for k in range(KC):
                    last = pe.transpose(ps_rows[:, a, k, :], rows[a][:, k * P:(k + 1) * P], ident[:])
                last.then_inc(rows_turned, 1)

            def up(g, e):
                wait(pe, g_lo_done, 2 * g + 2)
                for f in range(FC):
                    wait(pe, gelu_done, 2 * g - 1 + f if not isinstance(g, int) or g else 0)
                    for k in range(KC):
                        at = e * KC * F + k * F + f * P
                        last = split_product(ps_hid[:, f, 0:SLOTS], (w_hi[:, at:at + P], w_lo[:, at:at + P]),
                                             (g_hi[:, k, :], g_lo[:, k, :]), k == 0, k == KC - 1)
                    last.then_inc(up_done, 1)

            def down(g, a, e):
                pe.wait_ge(h_lo_done, 2 * g + a + 1)
                pe.wait_ge(y_biased, 2 * g + a + 1)
                slots = slice(a * P, (a + 1) * P)
                for f in range(FC):
                    at = W2_AT + e * FC * D + f * D
                    last = split_product(ps_y[:, a, :], (h_hi[:, f, slots], h_lo[:, f, slots]),
                                         (w_hi[:, at:at + D], w_lo[:, at:at + D]), f == 0, f == FC - 1)
                last.then_inc(down_done, 1)

            pe.wait_ge(xc_done, NT)
            for a in range(2):
                turn_rows(0, a)
            make_lists(B - 1, range(1, E))
            pe.wait_ge(w_hi_done, NT)
            pe.wait_ge(w_lo_done, NT)

            def stage(g, e, e_before):
                up(g, e)
                for a in range(2):
                    turn_rows(g + 1, a)
                if not isinstance(g, int):
                    for a in range(2):
                        down(g - 1, a, e_before)

            g = over_tiles(pe, stage, E + 1)
            for a in range(2):
                down(g - 1, a, E - 1)


def kernel(**inputs):
    import numpy as np
    import concourse.bacc as bacc
    from concourse.bass_utils import run_bass_kernel_spmd

    x = np.asarray(inputs["x"])
    Bn, S, D = x.shape
    T = Bn * S
    w_base = np.asarray(inputs["L0_cond_W_base"])
    a_mat = np.asarray(inputs["L0_cond_As"])
    b_mat = np.asarray(inputs["L0_cond_Bs"])
    w1 = np.asarray(inputs["L0_ffn_w1"])
    w2 = np.asarray(inputs["L0_ffn_w2"])
    E, _, F = w1.shape
    rank = a_mat.shape[1]
    KC, FC, NT = D // P, F // P, T // P

    consts = np.zeros((P, 3 * P + NT), np.float32)
    consts[:, IDENT:IDENT + P] = np.eye(P)
    consts[:, TRI:TRI + P] = np.triu(np.ones((P, P)), 1)
    consts[:, IOTA:IOTA + P] = np.arange(P)
    consts[:, TOKEN:TOKEN + NT] = (np.arange(T) - T // 2).reshape(NT, P).T

    arrays = {
        "xT": x.reshape(NT, P, KC, P).transpose(0, 3, 2, 1).reshape(T, D),
        "x": x.reshape(T, D),
        "consts": consts,
        "cond": np.repeat(np.asarray(inputs["cond_8"]).T, rank, axis=0),
        "base_wT": w_base.T.reshape(KC, P, D).transpose(1, 0, 2).reshape(P, KC * D),
        "base_w": w_base.reshape(KC, P, D).transpose(1, 0, 2).reshape(P, KC * D),
        "base_b": np.asarray(inputs["L0_cond_b_base"]),
        "base_bT": np.asarray(inputs["L0_cond_b_base"]).reshape(KC, P).T,
        "lora_a": a_mat.reshape(E * rank, D),
        "lora_b": b_mat.transpose(0, 2, 1).reshape(E * rank, D),
        "lora_bT": b_mat.transpose(1, 0, 2).reshape(KC, P, E * rank).transpose(1, 0, 2).reshape(P, KC * E * rank),
        "weights": np.concatenate([
            w1.reshape(E, KC, P, F).transpose(2, 0, 1, 3).reshape(P, E * KC * F),
            w2.reshape(E, FC, P, D).transpose(2, 0, 1, 3).reshape(P, E * FC * D)], axis=1),
        "b1": np.asarray(inputs["L0_ffn_b1"]).reshape(E, FC, P).transpose(2, 0, 1).reshape(P, E * FC),
        "b2": np.asarray(inputs["L0_ffn_b2"]),
        "centroids": np.asarray(inputs["L0_ffn_centroids"]),
        "w_route": np.asarray(inputs["L0_ffn_w_route"]),
    }
    nc = bacc.Bacc("TRN2", target_bir_lowering=False, num_devices=1)
    feeds, args = {}, []
    for name, a in arrays.items():
        a = np.ascontiguousarray(a)
        feeds[f"in_{name}"] = a
        args.append(nc.dram_tensor(f"in_{name}", a.shape, mybir.dt.from_np(a.dtype), kind="ExternalInput").ap())
    out = nc.dram_tensor("out_0", (T, D), F32, kind="ExternalOutput").ap()
    adaln_moe(nc, *args, out)
    r = run_bass_kernel_spmd(nc, [feeds], core_ids=[0])
    return r.results[0]["out_0"].reshape(Bn, S, D)
```
